# Optimizing a Trainium2 kernel written in Bass

```python
import numpy as np
import jax
import jax.numpy as jnp

def _softmax(x, axis=-1):
    return jax.nn.softmax(x, axis=axis)

def _gelu(x):
    return jax.nn.gelu(x, approximate=True)

def _silu(x):
    return jax.nn.silu(x)

def _sigmoid(x):
    return jax.nn.sigmoid(x)

def _layernorm(x, axis=-1, eps=1e-05):
    m = jnp.mean(x, axis=axis, keepdims=True)
    v = jnp.var(x, axis=axis, keepdims=True)
    return (x - m) / jnp.sqrt(v + eps)

def _scatter_add(tgt, idx, src, axis=0):
    return tgt.at[idx].add(src)

def _segment_sum(src, seg, n):
    return jax.ops.segment_sum(src, seg, n)
kernel_name = 'mk_dlrm_tower_d1_rec_r8_34af9f'

def setup_inputs(seed: int=0):
    np.random.seed(seed)
    _w = jnp.asarray

    def _rec_inputs():
        import jax
        import jax.numpy as jnp
        _tk = jax.random.key(seed)
        dense_ctx = jax.random.normal(jax.random.fold_in(_tk, 190), (512, 16), jnp.float32)
        ids = jnp.stack([jax.random.randint(jax.random.fold_in(_tk, 200 + f), (512,), 0, v, jnp.int32) for f, v in enumerate([125000, 1000, 125000, 1000, 125000, 1000, 12500, 1000, 1250, 125000, 1000, 1000, 12500, 1250, 1000, 1000, 1250, 1000, 125000, 12500, 125000, 1000, 1250, 125000])], axis=1)
        tbl_0 = 0.05 * jax.random.normal(jax.random.fold_in(_tk, 500 + 0), (125000, 16), jnp.float32)
        tbl_1 = 0.05 * jax.random.normal(jax.random.fold_in(_tk, 500 + 1), (1000, 16), jnp.float32)
        tbl_2 = 0.05 * jax.random.normal(jax.random.fold_in(_tk, 500 + 2), (125000, 16), jnp.float32)
        tbl_3 = 0.05 * jax.random.normal(jax.random.fold_in(_tk, 500 + 3), (1000, 16), jnp.float32)
        tbl_4 = 0.05 * jax.random.normal(jax.random.fold_in(_tk, 500 + 4), (125000, 16), jnp.float32)
        tbl_5 = 0.05 * jax.random.normal(jax.random.fold_in(_tk, 500 + 5), (1000, 16), jnp.float32)
        tbl_6 = 0.05 * jax.random.normal(jax.random.fold_in(_tk, 500 + 6), (12500, 16), jnp.float32)
        tbl_7 = 0.05 * jax.random.normal(jax.random.fold_in(_tk, 500 + 7), (1000, 16), jnp.float32)
        tbl_8 = 0.05 * jax.random.normal(jax.random.fold_in(_tk, 500 + 8), (1250, 16), jnp.float32)
        tbl_9 = 0.05 * jax.random.normal(jax.random.fold_in(_tk, 500 + 9), (125000, 16), jnp.float32)
        tbl_10 = 0.05 * jax.random.normal(jax.random.fold_in(_tk, 500 + 10), (1000, 16), jnp.float32)
        tbl_11 = 0.05 * jax.random.normal(jax.random.fold_in(_tk, 500 + 11), (1000, 16), jnp.float32)
        tbl_12 = 0.05 * jax.random.normal(jax.random.fold_in(_tk, 500 + 12), (12500, 16), jnp.float32)
        tbl_13 = 0.05 * jax.random.normal(jax.random.fold_in(_tk, 500 + 13), (1250, 16), jnp.float32)
        tbl_14 = 0.05 * jax.random.normal(jax.random.fold_in(_tk, 500 + 14), (1000, 16), jnp.float32)
        tbl_15 = 0.05 * jax.random.normal(jax.random.fold_in(_tk, 500 + 15), (1000, 16), jnp.float32)
        tbl_16 = 0.05 * jax.random.normal(jax.random.fold_in(_tk, 500 + 16), (1250, 16), jnp.float32)
        tbl_17 = 0.05 * jax.random.normal(jax.random.fold_in(_tk, 500 + 17), (1000, 16), jnp.float32)
        tbl_18 = 0.05 * jax.random.normal(jax.random.fold_in(_tk, 500 + 18), (125000, 16), jnp.float32)
        tbl_19 = 0.05 * jax.random.normal(jax.random.fold_in(_tk, 500 + 19), (12500, 16), jnp.float32)
        tbl_20 = 0.05 * jax.random.normal(jax.random.fold_in(_tk, 500 + 20), (125000, 16), jnp.float32)
        tbl_21 = 0.05 * jax.random.normal(jax.random.fold_in(_tk, 500 + 21), (1000, 16), jnp.float32)
        tbl_22 = 0.05 * jax.random.normal(jax.random.fold_in(_tk, 500 + 22), (1250, 16), jnp.float32)
        tbl_23 = 0.05 * jax.random.normal(jax.random.fold_in(_tk, 500 + 23), (125000, 16), jnp.float32)
        _rk = jax.random.fold_in(_tk, 7)
        W_top1 = 0.0693375 * jax.random.normal(jax.random.fold_in(_tk, 801), (208, 512), jnp.float32)
        W_top2 = 0.0441942 * jax.random.normal(jax.random.fold_in(_tk, 802), (512, 256), jnp.float32)
        W_top3 = 0.0625 * jax.random.normal(jax.random.fold_in(_tk, 803), (256, 1), jnp.float32)
        b_top1 = jnp.zeros((512,), jnp.float32)
        b_top2 = jnp.zeros((256,), jnp.float32)
        return (dense_ctx, ids, tbl_0, tbl_1, tbl_2, tbl_3, tbl_4, tbl_5, tbl_6, tbl_7, tbl_8, tbl_9, tbl_10, tbl_11, tbl_12, tbl_13, tbl_14, tbl_15, tbl_16, tbl_17, tbl_18, tbl_19, tbl_20, tbl_21, tbl_22, tbl_23, W_top1, b_top1, W_top2, b_top2, W_top3)
    dense_ctx, ids, tbl_0, tbl_1, tbl_2, tbl_3, tbl_4, tbl_5, tbl_6, tbl_7, tbl_8, tbl_9, tbl_10, tbl_11, tbl_12, tbl_13, tbl_14, tbl_15, tbl_16, tbl_17, tbl_18, tbl_19, tbl_20, tbl_21, tbl_22, tbl_23, W_top1, b_top1, W_top2, b_top2, W_top3 = _rec_inputs()

    def _L0_rec_setup():
        import jax, jax.numpy as jnp
        import numpy as np
        B, F, D = (512, 24, 16)
        LAYER_SIZES = [64, 64, 64]

        def _cin_forward(X0, Ws):
            F_ = X0.shape[1]
            Xk = X0
            outs = []
            for W in Ws:
                H_prev = Xk.shape[1]
                Wr = W.reshape(F_, H_prev, W.shape[1])
                Xk = jnp.einsum('bfd,bhd,fho->bod', X0, Xk, Wr)
                outs.append(Xk.sum(axis=2))
            return jnp.concatenate(outs, axis=1)
        key = jax.random.key(seed)
        k0, k1, k2, k3 = jax.random.split(key, 4)
        X0 = jax.random.normal(k0, (B, F, D), dtype=jnp.float32)
        prev = F
        Ws = []
        for k, h in zip((k1, k2, k3), LAYER_SIZES):
            Ws.append(jax.random.normal(k, (prev * F, h), dtype=jnp.float32) * 0.01)
            prev = h
        return {'X0': X0, 'W0': Ws[0], 'W1': Ws[1], 'W2': Ws[2]}
    _L0_rec_all = _L0_rec_setup()
    _L0_rec_in = {k: v for k, v in _L0_rec_all.items() if k in ('W0', 'W1', 'W2')}
    del _L0_rec_all
    return {'dense_ctx': dense_ctx, 'ids': ids, 'tbl_0': tbl_0, 'tbl_1': tbl_1, 'tbl_2': tbl_2, 'tbl_3': tbl_3, 'tbl_4': tbl_4, 'tbl_5': tbl_5, 'tbl_6': tbl_6, 'tbl_7': tbl_7, 'tbl_8': tbl_8, 'tbl_9': tbl_9, 'tbl_10': tbl_10, 'tbl_11': tbl_11, 'tbl_12': tbl_12, 'tbl_13': tbl_13, 'tbl_14': tbl_14, 'tbl_15': tbl_15, 'tbl_16': tbl_16, 'tbl_17': tbl_17, 'tbl_18': tbl_18, 'tbl_19': tbl_19, 'tbl_20': tbl_20, 'tbl_21': tbl_21, 'tbl_22': tbl_22, 'tbl_23': tbl_23, 'W_top1': W_top1, 'b_top1': b_top1, 'W_top2': W_top2, 'b_top2': b_top2, 'W_top3': W_top3, 'L0_rec_W0': _L0_rec_in['W0'], 'L0_rec_W1': _L0_rec_in['W1'], 'L0_rec_W2': _L0_rec_in['W2']}

def reference(dense_ctx, ids, tbl_0, tbl_1, tbl_2, tbl_3, tbl_4, tbl_5, tbl_6, tbl_7, tbl_8, tbl_9, tbl_10, tbl_11, tbl_12, tbl_13, tbl_14, tbl_15, tbl_16, tbl_17, tbl_18, tbl_19, tbl_20, tbl_21, tbl_22, tbl_23, W_top1, b_top1, W_top2, b_top2, W_top3, L0_rec_W0, L0_rec_W1, L0_rec_W2):
    import jax
    import jax.numpy as jnp

    def _L0_rec_ref(X0, W0, W1, W2):
        import jax, jax.numpy as jnp
        import numpy as np
        B, F, D = (512, 24, 16)
        LAYER_SIZES = [64, 64, 64]

        def _cin_forward(X0, Ws):
            F_ = X0.shape[1]
            Xk = X0
            outs = []
            for W in Ws:
                H_prev = Xk.shape[1]
                Wr = W.reshape(F_, H_prev, W.shape[1])
                Xk = jnp.einsum('bfd,bhd,fho->bod', X0, Xk, Wr)
                outs.append(Xk.sum(axis=2))
            return jnp.concatenate(outs, axis=1)
        return _cin_forward(X0, (W0, W1, W2))
    e = jnp.stack([tbl_0[ids[:, 0]], tbl_1[ids[:, 1]], tbl_2[ids[:, 2]], tbl_3[ids[:, 3]], tbl_4[ids[:, 4]], tbl_5[ids[:, 5]], tbl_6[ids[:, 6]], tbl_7[ids[:, 7]], tbl_8[ids[:, 8]], tbl_9[ids[:, 9]], tbl_10[ids[:, 10]], tbl_11[ids[:, 11]], tbl_12[ids[:, 12]], tbl_13[ids[:, 13]], tbl_14[ids[:, 14]], tbl_15[ids[:, 15]], tbl_16[ids[:, 16]], tbl_17[ids[:, 17]], tbl_18[ids[:, 18]], tbl_19[ids[:, 19]], tbl_20[ids[:, 20]], tbl_21[ids[:, 21]], tbl_22[ids[:, 22]], tbl_23[ids[:, 23]]], axis=1)
    z = _L0_rec_ref(e, L0_rec_W0, L0_rec_W1, L0_rec_W2)
    z = z.reshape(z.shape[0], -1)
    h = jnp.concatenate([z, dense_ctx], axis=1)
    h = jnp.maximum(h @ W_top1 + b_top1, 0.0)
    h = jnp.maximum(h @ W_top2 + b_top2, 0.0)
    y = h @ W_top3
    return y

_drawn_inputs = setup_inputs


def setup_inputs(seed=0):
    import zlib

    import numpy as np

    out = dict(_drawn_inputs(seed))
    spreads = {'b_top1': (0.0, 0.1), 'b_top2': (0.0, 0.1)}
    factors = {'tbl_0': 8.0,
     'tbl_1': 8.0,
     'tbl_2': 8.0,
     'tbl_3': 8.0,
     'tbl_4': 8.0,
     'tbl_5': 8.0,
     'tbl_6': 8.0,
     'tbl_7': 8.0,
     'tbl_8': 8.0,
     'tbl_9': 8.0,
     'tbl_10': 8.0,
     'tbl_11': 8.0,
     'tbl_12': 8.0,
     'tbl_13': 8.0,
     'tbl_14': 8.0,
     'tbl_15': 8.0,
     'tbl_16': 8.0,
     'tbl_17': 8.0,
     'tbl_18': 8.0,
     'tbl_19': 8.0,
     'tbl_20': 8.0,
     'tbl_21': 8.0,
     'tbl_22': 8.0,
     'tbl_23': 8.0,
     'L0_rec_W0': 8.0,
     'L0_rec_W1': 8.0,
     'L0_rec_W2': 8.0}
    for name, (base, spread) in spreads.items():
        noise = np.random.default_rng([zlib.crc32(name.encode()), seed]).standard_normal(out[name].shape)
        drawn = base * np.exp(spread * noise) if base else spread * noise
        out[name] = jnp.asarray(drawn.astype(out[name].dtype))
    for name, factor in factors.items():
        out[name] = (out[name] * factor).astype(out[name].dtype)
    return out
```

```python
import concourse.bass as bass
from concourse import mybir
from contextlib import ExitStack

import numpy as np

F32 = mybir.dt.float32
BF16 = mybir.dt.bfloat16
I32 = mybir.dt.int32
ALU = mybir.AluOpType
ACT = mybir.ActivationFunctionType
AX = mybir.AxisListType

B, F, D, H = 512, 24, 16, 64
PARTS = 3
XP = PARTS * F
TILE_B = 128
TILES = B // TILE_B
UNIT_B = 64
UNITS = B // UNIT_B
GB = 8
GROUPS = UNIT_B // GB
CG = GROUPS // 2
CHUNK = CG * GB * D
FH = F // 2
PAIRS = F * (F + 1) // 2
PT = 3
PR = PAIRS // PT
W0K = 6
W0R = F * F // W0K
GF = (FH + 1) * GB
D_CTX, N1, N2 = 16, 512, 256
C_PAIR, C_SPREAD, C_JOIN, C_EYE = 0, PAIRS, PAIRS + FH * 128, PAIRS + FH * 128 + F
C_BF = C_EYE + 128
C_F32 = 128 + GB


def dlrm_tower(nc, a, out):
    ctx = ExitStack()
    with ctx:
        def sb(name, shape, dt=F32):
            return ctx.enter_context(nc.sbuf_tensor(name, shape, dt))

        def ps(name):
            return ctx.enter_context(nc.psum_tensor(name, [128, 512], F32))

        def sem(name):
            return ctx.enter_context(nc.semaphore(name))

        ids = sb("ids_sb", [128, TILES, F], I32)
        emb = sb("emb", [128, TILES, F * D])
        cbf_f32 = sb("cbf_f32", [128, C_BF])
        cbf = sb("cbf", [128, C_BF], BF16)
        cf = sb("cf", [128, C_F32])
        fold = sb("fold", [W0R, W0K, PAIRS])
        w0 = sb("w0", [W0R, W0K, H])
        w0p = sb("w0p", [PR, PT, H])
        w1 = sb("w1", [128, FH, H])
        w2 = sb("w2", [128, FH, H])
        wt1a = sb("wt1a", [128, N1])
        wt1b = sb("wt1b", [H + D_CTX, N1])
        wt2 = sb("wt2", [128, N1 // 128, N2])
        wt3 = sb("wt3", [128, N2 // 128])
        b1 = sb("b1", [128, N1 // 128])
        b2 = sb("b2", [128, N2 // 128])
        rest1 = sb("rest1", [128, F * D])
        xs = sb("xs", [128, D, XP], BF16)
        xt = sb("xt", [XP, 2, GROUPS * 128], BF16)
        xdiag = sb("xdiag", [128, 2, GROUPS, F + 1, GB])
        sq = sb("sq", [PR, PT, 2, CHUNK])
        x1 = sb("x1", [128, 2, 2, CHUNK])
        prod = sb("prod", [128, 3, 2, CHUNK])
        x2 = sb("x2", [128, CHUNK])
        x2t = sb("x2t", [128, CG, 128])
        gram = sb("gram", [128, UNITS * FH * UNIT_B])
        z12 = sb("z12", [128, B])
        z3d = sb("z3d", [H + D_CTX, B])
        h1 = sb("h1", [128, N1 // 128, B])
        h2 = sb("h2", [128, N2 // 128, B])
        y = sb("y", [1, B])

        spread_ps = [ps(f"spread{i}") for i in range(4)]
        x2_ps, x1_ps, pair_ps, misc = ps("x2_ps"), ps("x1_ps"), ps("pair_ps"), ps("misc")
        misc_bf = misc[:, :].bitcast(BF16)

        ids_in, cbf_in, cbf_done, cf_in, w0_in, w1_in, w2_in = (sem(n) for n in (
            "ids_in", "cbf_in", "cbf_done", "cf_in", "w0_in", "w1_in", "w2_in"))
        top_in, ctx_in, ones_in = sem("top_in"), sem("ctx_in"), sem("ones_in")
        gathered = [sem(f"gathered{k}") for k in range(TILES)]
        split_step, split_done = sem("split_step"), sem("split_done")
        w0p_mm, w0p_done = sem("w0p_mm"), sem("w0p_done")
        xt_mm, xt_done = sem("xt_mm"), sem("xt_done")
        join_mm, xdiag_done = sem("join_mm"), sem("xdiag_done")
        pair_mm, sq_done = sem("pair_mm"), sem("sq_done")
        x1_mm, x1_done, z1_done = sem("x1_mm"), sem("x1_done"), sem("z1_done")
        spread_mm, prod_done, x2_mm, x2_done = sem("spread_mm"), sem("prod_done"), sem("x2_mm"), sem("x2_done")
        x2t_mm, x2t_done = sem("x2t_mm"), sem("x2t_done")
        gram_mm, gram_done = sem("gram_mm"), sem("gram_done")
        z3_mm, z3_done = sem("z3_mm"), sem("z3_done")
        h1_mm, h1_act, h1_dve = sem("h1_mm"), sem("h1_act"), sem("h1_dve")
        h2_mm, h2_act, h2_dve = sem("h2_mm"), sem("h2_act"), sem("h2_dve")
        y_mm, y_done, stored = sem("y_mm"), sem("y_done"), sem("stored")

        eye_f = cf[:, 0:128]
        block_mask = cf[:, 128:128 + GB]

        block = ctx.enter_context(nc.Block())

        @block.sync
        def _(sp):
            sp.dma_start(ids[:, :, :], a["ids"].rearrange("(t p) f -> p t f", p=TILE_B)).then_inc(ids_in, 16)
            sp.dma_start(fold[:, :, :], a["const_fold"].rearrange("(k p) n -> p k n", p=W0R)).then_inc(w0_in, 16)
            sp.dma_start(w0[:, :, :], a["L0_rec_W0"].rearrange("(k p) o -> p k o", p=W0R)).then_inc(w0_in, 16)
            sp.dma_start(cf[:, :], a["const_f32"][:, :]).then_inc(cf_in, 16)
            for w, name, got in ((w1, "L0_rec_W1", w1_in), (w2, "L0_rec_W2", w2_in)):
                rows = a[name].rearrange("(q t h) o -> q h t o", q=2, t=FH)
                for q in range(2):
                    sp.dma_start(w[H * q:H * q + H, :, :], rows[q]).then_inc(got, 16)
            sp.wait_ge(y_done, 1)
            sp.dma_start(out.rearrange("b o -> o b"), y[:, :]).then_inc(stored, 16)
            sp.wait_ge(stored, 16)

        @block.gpsimd
        def _(pool):
            for p in range(2):
                if p == 0:
                    pool.wait_ge(cf_in, 16)
                for g in range(GROUPS):
                    nc.gpsimd.tensor_copy(xdiag[:, p, g, F, :], block_mask).then_inc(ones_in, 1)
            pool.wait_ge(ids_in, 16)
            for k in range(TILES):
                for f in range(F):
                    nc.gpsimd.indirect_dma_start(
                        out=emb[:, k, f * D:(f + 1) * D], out_offset=None, in_=a[f"tbl_{f}"][:, :],
                        in_offset=bass.IndirectOffsetOnAxis(ap=ids[:, k, f:f + 1], axis=0),
                    ).then_inc(gathered[k], 16)

        @block.tensor
        def _(pe):
            def pair_sum(i, xt_half):
                k, c = i // 2, i % 2
                nc.tensor.matmul(pair_ps[0:PR, :], cbf[0:XP, C_PAIR + PR * k:C_PAIR + PR * (k + 1)],
                                 xt[:, xt_half, CHUNK * c:CHUNK * (c + 1)], start=True, stop=True).then_inc(pair_mm, 1)

            def spread(v, t, half):
                for c in range(2):
                    nc.tensor.matmul(spread_ps[2 * (t % 2) + c][:, :],
                                     cbf[0:XP, C_SPREAD + 128 * t:C_SPREAD + 128 * (t + 1)],
                                     xt[:, half, CHUNK * c:CHUNK * (c + 1)], start=True, stop=True).then_inc(spread_mm, 1)

            def back(w, half, t, with_front, last_unit=False):
                if t == 0:
                    pe.wait_ge(x2_done, w + 1)
                    pe.wait_ge(xdiag_done, w + 1)
                    if not last_unit:
                        pe.wait_ge(xdiag_done, w + 2)
                    for g in range(CG):
                        last = nc.tensor.transpose(misc[:, 128 * g:128 * (g + 1)], x2[:, 128 * g:128 * (g + 1)], eye_f)
                    last.then_inc(x2t_mm, 1)
                if t in (2, 4):
                    c = (t - 2) // 2
                    pe.wait_ge(x2t_done, w + 1)
                    if c == 0 and with_front:
                        pe.wait_ge(xt_done, w + 3)
                    if c == 1:
                        pe.wait_ge(gram_done, 2 * w + 1)
                    for g in range(CG):
                        for q in range(2):
                            n = (FH + q) * GB
                            last = nc.tensor.matmul(
                                misc[H * q:H * q + H, GF * g:GF * g + n], x2t[:, g, H * c:H * c + H],
                                xdiag[:, half, CG * c + g, FH * q:FH * q + FH + q, :].rearrange("p f b -> p (f b)"),
                                start=True, stop=True)
                    last.then_inc(gram_mm, 1)

            def front(v, half, rows, t, behind):
                if t == 1:
                    if behind:
                        pe.wait_ge(x2t_done, v - 1)
                    elif v > 0:
                        pe.wait_ge(xdiag_done, v)
                    for d in range(D):
                        last = nc.tensor.transpose(misc_bf[0:XP, UNIT_B * d:UNIT_B * (d + 1)], xs[rows:rows + UNIT_B, d, :],
                                                   cbf[rows:rows + UNIT_B, C_EYE + rows:C_EYE + rows + UNIT_B])
                    last.then_inc(xt_mm, 1)
                if t == 2:
                    pe.wait_ge(xt_done, v + 1)
                if 2 <= t <= 7:
                    i = t - 2
                    if i or behind or not isinstance(v, int) or v > 0:
                        pe.wait_ge(sq_done, 6 * v + i)
                    pair_sum(i, half)
                if t == 5:
                    if behind:
                        pe.wait_ge(gram_done, 2 * v - 2)
                    for g in range(GROUPS):
                        last = nc.tensor.matmul(misc[:, F * g:F * (g + 1)], xt[:, half, 128 * g:128 * (g + 1)],
                                                cbf[0:XP, C_JOIN:C_JOIN + F], start=True, stop=True)
                    last.then_inc(join_mm, 1)
                if t in (5, 7, 9):
                    k = (t - 5) // 2
                    pe.wait_ge(sq_done, 6 * v + 2 * k + 2)
                    if k == 0 and not (isinstance(v, int) and v == 0):
                        pe.wait_ge(x1_done, 4 * v)
                    for c in range(2):
                        last = nc.tensor.matmul(x1_ps[H * c:H * c + H, :], w0p[:, k, :], sq[:, k, c, :],
                                                start=(k == 0), stop=(k == PT - 1))
                    if k == PT - 1:
                        last.then_inc(x1_mm, 1)

            def unit(u, half, is_first, is_last):
                for t in range(FH):
                    n = FH * u + t
                    pe.wait_ge(prod_done, 2 * n + 2)
                    if t == FH - 2 and not is_last:
                        pe.wait_ge(xt_done, u + 2)
                    if t < FH - 2:
                        spread(u, t + 2, half)
                    elif not is_last:
                        spread(u + 1, t + 2 - FH, 1 - half)
                    if t == 0 and not is_first:
                        pe.wait_ge(x2_done, u)
                    for c in range(2):
                        last = nc.tensor.matmul(x2_ps[H * c:H * c + H, :], w1[:, t, :], prod[:, t % 3, c, :],
                                                start=(t == 0), stop=(t == FH - 1))
                    last.then_inc(x2_mm, 1)
                    if not is_first:
                        back(u - 1, 1 - half, t, not is_last)
                    if not is_last:
                        if t == 1 and half == 1:
                            pe.wait_ge(split_done, (u + 3) // 2)
                        front(u + 1, 1 - half, UNIT_B * (1 - half), t, not is_first)

            pe.wait_ge(w0_in, 32)
            for k in range(PT):
                for r in range(W0K):
                    last = nc.tensor.matmul(misc[0:PR, H * k:H * (k + 1)], fold[:, r, PR * k:PR * (k + 1)], w0[:, r, :],
                                            start=(r == 0), stop=(r == W0K - 1))
            last.then_inc(w0p_mm, 1)
            pe.wait_ge(cbf_done, 1)
            pe.wait_ge(cf_in, 16)
            pe.wait_ge(ones_in, 2 * GROUPS)
            pe.wait_ge(w0p_done, 1)
            pe.wait_ge(split_done, 1)
            for t in range(10):
                front(0, 0, 0, t, False)
            pe.wait_ge(w1_in, 32)
            for t in range(2):
                spread(0, t, 0)
            for u in range(UNITS):
                unit(u, u % 2, u == 0, u == UNITS - 1)
            for t in range(5):
                back(UNITS - 1, (UNITS - 1) % 2, t, False, True)

            pe.wait_ge(w2_in, 32)
            pe.wait_ge(gram_done, 2 * UNITS)
            pe.wait_ge(x1_done, 4 * UNITS)
            g_all = gram[:, :].rearrange("p (u f b) -> p f u b", f=FH, b=UNIT_B)
            for t in range(FH):
                for s in range(2):
                    last = nc.tensor.matmul(x1_ps[H * s:H * s + H, 0:B // 2], w2[:, t, :],
                                            g_all[:, t, UNITS // 2 * s:UNITS // 2 * (s + 1), :],
                                            start=(t == 0), stop=(t == FH - 1))
            last.then_inc(z3_mm, 1)
            pe.wait_ge(top_in, 16 * 6)
            pe.wait_ge(ctx_in, 32)
            pe.wait_ge(z1_done, UNITS)
            for m in range(N1 // 128):
                nc.tensor.matmul(spread_ps[m][:, :], wt1a[:, 128 * m:128 * (m + 1)], z12[:, :], start=True, stop=False)
            pe.wait_ge(z3_done, 2)
            for m in range(N1 // 128):
                nc.tensor.matmul(spread_ps[m][:, :], wt1b[:, 128 * m:128 * (m + 1)], z3d[:, :], start=False,
                                 stop=True).then_inc(h1_mm, 1)
            h2_ps = (x2_ps, pair_ps)
            for k in range(N1 // 128):
                pe.wait_ge((h1_act, h1_dve)[k % 2], k // 2 + 1)
                for m in range(N2 // 128):
                    last = nc.tensor.matmul(h2_ps[m][:, :], wt2[:, k, 128 * m:128 * (m + 1)], h1[:, k, :],
                                            start=(k == 0), stop=(k == N1 // 128 - 1))
                    if k == N1 // 128 - 1:
                        last.then_inc(h2_mm, 1)
            for k in range(N2 // 128):
                pe.wait_ge((h2_act, h2_dve)[k % 2], 1)
                last = nc.tensor.matmul(misc[0:1, :], wt3[:, k:k + 1], h2[:, k, :], start=(k == 0), stop=(k == N2 // 128 - 1))
            last.then_inc(y_mm, 1)

        @block.scalar
        def _(act):
            act.dma_start(cbf_f32[:, :], a["const_sel"][:, :]).then_inc(cbf_in, 16)
            act.dma_start(wt1a[:, :], a["W_top1"][0:128, :]).then_inc(top_in, 16)
            act.dma_start(wt1b[0:H, :], a["W_top1"][128:128 + H, :]).then_inc(top_in, 16)
            act.dma_start(wt1b[H:H + D_CTX, :], a["W_top1"][128 + H:, :]).then_inc(top_in, 16)
            act.dma_start(wt2[:, :, :], a["W_top2"].rearrange("(k p) n -> p k n", p=128)).then_inc(top_in, 16)
            act.dma_start(wt3[:, :], a["W_top3"][:, :]).then_inc(top_in, 16)
            act.dma_start(b1[:, :], a["b_top1"][:, :]).then_inc(top_in, 16)
            act.dma_start(b2[:, :], a["b_top2"][:, :]).then_inc(ctx_in, 16)
            act.dma_start(z3d[H:H + D_CTX, :], a["dense_t"][:, :]).then_inc(ctx_in, 16)

            def copy(o, i):
                return nc.scalar.activation(o, i, ACT.Copy)

            def x2_copy(w):
                act.wait_ge(x2_mm, FH * (w + 1))
                copy(x2[:, :], x2_ps[:, :]).then_inc(x2_done, 1)

            def back(w, t):
                if t == 0:
                    act.wait_ge(x2t_mm, w + 1)
                    copy(x2t[:, :, :].rearrange("p g m -> p (g m)"), misc[:, :]).then_inc(x2t_done, 1)
                if t in (2, 4):
                    c = (t - 2) // 2
                    act.wait_ge(gram_mm, 2 * w + c + 1)
                    sums = misc[:, 0:CG * GF].rearrange("p (g f b) -> p g f b", g=CG, b=GB)
                    here = gram[:, bass.ds(w * FH * UNIT_B, FH * UNIT_B)]
                    here = here.rearrange("p (f c g b) -> p c g f b", f=FH, c=2, g=CG)
                    copy(here[:, c], sums[:, :, 0:FH, :])
                    zs = z12[H:2 * H, bass.ds(w * UNIT_B + c * CG * GB, CG * GB)]
                    copy(zs.rearrange("p (g b) -> p g b", g=CG), sums[H:2 * H, :, FH, :]).then_inc(gram_done, 1)

            def front(v, half, t):
                if t == 1:
                    act.wait_ge(xt_mm, v + 1)
                    copy(xt[:, half, :].rearrange("p (g d b) -> p g d b", g=GROUPS, d=D),
                         misc_bf[0:XP, :].rearrange("p (d g b) -> p g d b", d=D, g=GROUPS)).then_inc(xt_done, 1)
                if 2 <= t <= 7:
                    i = t - 2
                    if i == 0 and not (isinstance(v, int) and v == 0):
                        act.wait_ge(x1_mm, v)
                    act.wait_ge(pair_mm, 6 * v + i + 1)
                    nc.scalar.activation(sq[:, i // 2, i % 2, :], pair_ps[0:PR, :], ACT.Square).then_inc(sq_done, 1)
                if t == 9:
                    act.wait_ge(x1_mm, v + 1)
                    for c in range(2):
                        for q in range(2):
                            copy(x1[H * q:H * q + H, half, c, :], x1_ps[H * c:H * c + H, :]).then_inc(x1_done, 1)

            act.wait_ge(w0p_mm, 1)
            copy(w0p[:, :, :].rearrange("p k o -> p (k o)"), misc[0:PR, 0:PT * H]).then_inc(w0p_done, 1)
            for t in range(10):
                front(0, 0, t)
            for u in range(UNITS):
                if u > 0:
                    x2_copy(u - 1)
                for t in range(FH):
                    if u > 0:
                        back(u - 1, t)
                    if u < UNITS - 1:
                        front(u + 1, (u + 1) % 2, t)
            x2_copy(UNITS - 1)
            for t in range(5):
                back(UNITS - 1, t)

            act.wait_ge(z3_mm, 1)
            for s in range(2):
                copy(z3d[0:H, B // 2 * s:B // 2 * (s + 1)], x1_ps[H * s:H * s + H, 0:B // 2]).then_inc(z3_done, 1)
            act.wait_ge(top_in, 16 * 6)
            act.wait_ge(ctx_in, 32)
            for m in (0, 2):
                act.wait_ge(h1_mm, m + 1)
                nc.scalar.activation(h1[:, m, :], spread_ps[m][:, :], ACT.Relu, bias=b1[:, m:m + 1]).then_inc(h1_act, 1)
            act.wait_ge(h2_mm, 1)
            nc.scalar.activation(h2[:, 0, :], x2_ps[:, :], ACT.Relu, bias=b2[:, 0:1]).then_inc(h2_act, 1)
            act.wait_ge(y_mm, 1)
            copy(y[:, :], misc[0:1, :]).then_inc(y_done, 1)

        @block.vector
        def _(dve):
            def split(k, step):
                parts = xs[:, :, :].rearrange("p d (s f) -> p s f d", s=PARTS)
                x = emb[:, k, :].rearrange("p (f d) -> p f d", d=D)
                r = rest1[:, :].rearrange("p (f d) -> p f d", d=D)
                if step == 0:
                    dve.wait_ge(gathered[k], 16 * F)
                    nc.vector.tensor_copy(parts[:, 0], x).then_inc(split_step, 1)
                if step == 1:
                    dve.wait_ge(split_step, 3 * k + 1)
                    nc.vector.tensor_tensor(r, x, parts[:, 0], ALU.subtract).then_inc(split_step, 1)
                if step == 2:
                    dve.wait_ge(split_step, 3 * k + 2)
                    nc.vector.tensor_copy(parts[:, 1], r).then_inc(split_step, 1)
                if step == 3:
                    dve.wait_ge(split_step, 3 * k + 3)
                    nc.vector.tensor_tensor(parts[:, 2], r, parts[:, 1], ALU.subtract).then_inc(split_done, 1)

            def front(v, half, t):
                if t == 7:
                    dve.wait_ge(join_mm, v + 1)
                    shape = [128, GROUPS, F, GB]
                    x = misc[:, 0:GROUPS * F].rearrange("p (g f) -> p g f", g=GROUPS)
                    nc.vector.tensor_tensor(xdiag[:, half, :, 0:F, :], x.unsqueeze(3).broadcast_to(shape),
                                            block_mask.unsqueeze(1).unsqueeze(1).broadcast_to(shape),
                                            ALU.mult).then_inc(xdiag_done, 1)

            def sum_x1(u, half):
                here = z12[0:H, bass.ds(u * UNIT_B, UNIT_B)].rearrange("p (g b) -> p g b", g=GROUPS)
                nc.vector.tensor_reduce(here, x1[0:H, half, :, :].rearrange("p c (g d b) -> p (c g) b d", g=CG, d=D),
                                        AX.X, ALU.add).then_inc(z1_done, 1)

            dve.wait_ge(cbf_in, 16)
            nc.vector.tensor_copy(cbf[:, :], cbf_f32[:, :]).then_inc(cbf_done, 1)
            for s in range(4):
                split(0, s)
            dve.wait_ge(cf_in, 16)
            for t in range(11):
                front(0, 0, t)
            for u in range(UNITS):
                for t in range(FH):
                    n = FH * u + t
                    if t == 0:
                        dve.wait_ge(x1_done, 4 * (u + 1))
                    for c in range(2):
                        dve.wait_ge(spread_mm, 2 * n + c + 1)
                        if n >= 3:
                            dve.wait_ge(x2_mm, n - 2)
                        nc.vector.tensor_tensor(prod[:, t % 3, c, :], spread_ps[2 * (t % 2) + c][:, :],
                                                x1[:, u % 2, c, :], ALU.mult).then_inc(prod_done, 1)
                    if t == 2:
                        sum_x1(u, u % 2)
                    if u < UNITS - 1:
                        front(u + 1, (u + 1) % 2, t)
                    if u % 2 == 0 and u // 2 + 1 < TILES and t >= FH - 4:
                        split(u // 2 + 1, t - (FH - 4))
            for m in (1, 3):
                dve.wait_ge(h1_mm, m + 1)
                nc.vector.tensor_scalar(h1[:, m, :], spread_ps[m][:, :], b1[:, m:m + 1], 0.0, ALU.add,
                                        ALU.max).then_inc(h1_dve, 1)
            dve.wait_ge(ctx_in, 32)
            dve.wait_ge(h2_mm, 2)
            nc.vector.tensor_scalar(h2[:, 1, :], pair_ps[:, :], b2[:, 1:2], 0.0, ALU.add, ALU.max).then_inc(h2_dve, 1)


def constants():
    pairs = [(i, j) for i in range(F) for j in range(i, F)]
    fold = np.zeros((F * F, PAIRS), np.float32)
    add = np.zeros((F, PAIRS), np.float32)
    for m, (i, j) in enumerate(pairs):
        add[i, m] = add[j, m] = 1
        if i != j:
            fold[i * F + j, m] = fold[j * F + i, m] = 0.5
        else:
            fold[i * F:(i + 1) * F, m] = -0.5
            fold[i::F, m] = -0.5
            fold[i * F + i, m] = 1
    spread = np.zeros((F, FH, 128), np.float32)
    for t in range(FH):
        spread[t, t, 0:H] = spread[t + FH, t, H:] = 1
    const_sel = np.zeros((128, C_BF), np.float32)
    const_sel[0:XP, C_PAIR:C_SPREAD] = np.tile(add, (PARTS, 1))
    const_sel[0:XP, C_SPREAD:C_JOIN] = np.tile(spread.reshape(F, -1), (PARTS, 1))
    const_sel[0:XP, C_JOIN:C_EYE] = np.tile(np.eye(F, dtype=np.float32), (PARTS, 1))
    const_sel[:, C_EYE:] = np.eye(128)
    const_f32 = np.zeros((128, C_F32), np.float32)
    const_f32[:, 0:128] = np.eye(128)
    const_f32[:, 128:] = np.tile(np.eye(GB), (D, 1))
    return fold, const_sel, const_f32


def kernel(**inputs):
    import concourse.bacc as bacc
    from concourse.bass_utils import run_bass_kernel_spmd as run

    nc = bacc.Bacc("TRN2", target_bir_lowering=False, num_devices=1)
    arrays = {n: np.ascontiguousarray(x) for n, x in inputs.items() if n != "dense_ctx"}
    arrays["dense_t"] = np.ascontiguousarray(np.asarray(inputs["dense_ctx"]).T)
    for name in ("W_top3", "b_top1", "b_top2"):
        arrays[name] = np.ascontiguousarray(arrays[name].reshape(-1, 128).T)
    arrays["const_fold"], arrays["const_sel"], arrays["const_f32"] = constants()
    args = {n: nc.dram_tensor(n, x.shape, mybir.dt.from_np(x.dtype), kind="ExternalInput").ap()
            for n, x in arrays.items()}
    out = nc.dram_tensor("out", (B, 1), F32, kind="ExternalOutput").ap()
    dlrm_tower(nc, args, out)
    r = run(nc, [arrays], core_ids=[0])
    return r.results[0]["out"]
```

```python
import concourse.bass as bass
from concourse import mybir
from contextlib import ExitStack

import numpy as np

F32 = mybir.dt.float32
BF16 = mybir.dt.bfloat16
I32 = mybir.dt.int32
ALU = mybir.AluOpType
ACT = mybir.ActivationFunctionType
AX = mybir.AxisListType

B, F, D, H = 512, 24, 16, 64
PARTS = 3
UNIT_B = 64
UNITS = B // UNIT_B
GB = 8
GROUPS = UNIT_B // GB
CG = GROUPS // 2
CHUNK = CG * GB * D
POS = 2 * CHUNK
FH = F // 2
TS = 3
DMA_STEPS = ((3, 6), (6, 9), (9, 12))
PAIRS = F * (F + 1) // 2
PT = 3
PR = PAIRS // PT
W0K = 6
W0R = F * F // W0K
GF = (FH + 1) * GB
RING = 4
FIRST_LATE = 3
D_CTX, N1, N2 = 16, 512, 256
M1, M2 = N1 // 128, N2 // 128
C_PAIR, C_SPREAD = 0, PAIRS
C_JOIN = C_SPREAD + TS * 128
C_EYE = C_JOIN + F
C_SEL = C_EYE + 64
C_F32 = 128 + GB
BATCHES = ((0, 6), (6, 2))


def dlrm_tower(nc, a, out):
    ctx = ExitStack()
    with ctx:
        def sb(name, shape, dt=F32):
            return ctx.enter_context(nc.sbuf_tensor(name, shape, dt))

        def ps(name, cols=512):
            return ctx.enter_context(nc.psum_tensor(name, [128, cols], F32))

        def sem(name):
            return ctx.enter_context(nc.semaphore(name))

        lookup = sb("lookup_sb", [128, (UNITS + 1) * FH], I32)
        rows = sb("rows", [128, UNITS, FH], I32)
        sel_f32 = sb("sel_f32", [128, C_SEL])
        sel = sb("sel", [128, C_SEL], BF16)
        cf = sb("cf", [128, C_F32])
        fold = sb("fold", [W0R, W0K, PAIRS])
        w0 = sb("w0", [W0R, W0K, H])
        w0p = sb("w0p", [PR, PT, H])
        w1 = sb("w1", [128, FH, H])
        w2 = sb("w2", [128, FH, H])
        wt1a = sb("wt1a", [128, N1])
        wt1b = sb("wt1b", [H + D_CTX, N1])
        wt2 = sb("wt2", [128, M1, N2])
        wt3 = sb("wt3", [128, M2])
        b1 = sb("b1", [128, M1])
        b2 = sb("b2", [128, M2])
        emb = sb("emb", [128, 2, FH * D])
        rest = sb("rest", [128, FH * D])
        xs = sb("xs", [128, D, 64], BF16)
        xt = sb("xt", [128, 2, POS], BF16)
        xf = sb("xf", [F, POS])
        xf_dram = nc.dram_tensor("xf_dram", (2, F, POS), F32, kind="Internal").ap()
        xspread = sb("xspread", [128, FH - TS, POS])
        xdiag = sb("xdiag", [128, 2, GROUPS, F + 1, GB])
        sq = sb("sq", [PR, PT, 2, CHUNK])
        x1 = sb("x1", [128, 2, POS])
        prod = sb("prod", [128, RING, POS])
        x2 = sb("x2", [128, CHUNK])
        x2t = sb("x2t", [128, CG, 128])
        gram = sb("gram", [128, UNITS * FH * UNIT_B])
        z12 = sb("z12", [128, B])
        z3d = sb("z3d", [H + D_CTX, B])
        h1 = sb("h1", [128, M1, B])
        h2 = sb("h2", [128, M2, B])
        y = sb("y", [1, B])

        spread_ps = [ps(f"spread{i}", POS) for i in range(2)]
        x2_ps, x1_ps, pair_ps, misc = ps("x2_ps"), ps("x1_ps"), ps("pair_ps"), ps("misc")
        misc_bf = misc[:, :].bitcast(BF16)

        ids_in, rows_done, sel_in, sel_done, cf_in = (sem(n) for n in (
            "ids_in", "rows_done", "sel_in", "sel_done", "cf_in"))
        w0_in, w1_in, w2_in, top_in, pad_done, ones_done = (sem(n) for n in (
            "w0_in", "w1_in", "w2_in", "top_in", "pad_done", "ones_done"))
        gathered = [sem("gathered_even"), sem("gathered_odd")]
        split_step, split_done = sem("split_step"), sem("split_done")
        w0p_mm, w0p_done = sem("w0p_mm"), sem("w0p_done")
        xt_mm, xt_done = sem("xt_mm"), sem("xt_done")
        xf_mm, xf_done, xf_stored = sem("xf_mm"), sem("xf_done"), sem("xf_stored")
        spread_in = [sem(f"spread_in{i}") for i in range(len(DMA_STEPS))]
        join_mm, xdiag_done = sem("join_mm"), sem("xdiag_done")
        pair_mm, sq_done = sem("pair_mm"), sem("sq_done")
        x1_mm, x1_done, z1_done = sem("x1_mm"), sem("x1_done"), sem("z1_done")
        spread_mm, prod_done, x2_mm, x2_done = sem("spread_mm"), sem("prod_done"), sem("x2_mm"), sem("x2_done")
        x2t_mm, x2t_done = sem("x2t_mm"), sem("x2t_done")
        gram_mm, gram_done = sem("gram_mm"), sem("gram_done")
        z3_mm, z3_half, z3_done, h1_mm, h1_done = sem("z3_mm"), sem("z3_half"), sem("z3_done"), sem("h1_mm"), sem("h1_done")
        h2_mm, h2_done, y_mm, y_done, stored = (sem(n) for n in ("h2_mm", "h2_done", "y_mm", "y_done", "stored"))

        eye_f = cf[:, 0:128]
        block_mask = cf[:, 128:128 + GB]
        spread_halves = [s[:, CHUNK * c:CHUNK * (c + 1)] for s in spread_ps for c in range(2)]
        pair_banks = [pair_ps[:, :]] + [spread_halves[i] for i in (2, 3, 0, 1, 2)]
        first_pairs = [pair_ps[:, :], x2_ps[:, :]] + spread_halves

        block = ctx.enter_context(nc.Block())

        def all_units(engine, unit):
            unit(0, 0, True, False)
            with engine.Fori(0, (UNITS - 2) // 2) as i:
                for s in range(2):
                    unit(2 * i + 1 + s, 1 - s, False, False)
            unit(UNITS - 1, 1, False, True)

        @block.sync
        def _(sp):
            sp.dma_start(lookup[:, :], a["lookup"][:, :]).then_inc(ids_in, 16)
            sp.dma_start(fold[:, :, :], a["const_fold"].rearrange("(k p) n -> p k n", p=W0R)).then_inc(w0_in, 16)
            sp.dma_start(w0[:, :, :], a["L0_rec_W0"].rearrange("(k p) o -> p k o", p=W0R)).then_inc(w0_in, 16)
            sp.dma_start(cf[:, :], a["const_f32"][:, :]).then_inc(cf_in, 16)
            for w, name, got in ((w1, "L0_rec_W1", w1_in), (w2, "L0_rec_W2", w2_in)):
                by_step = a[name].rearrange("(q t h) o -> q h t o", q=2, t=FH)
                for q in range(2):
                    sp.dma_start(w[H * q:H * q + H, :, :], by_step[q]).then_inc(got, 16)

            def spread(v, half, is_first):
                sp.wait_ge(xf_done, 2 * v + 2)
                sp.dma_start(xf_dram[half], xf[:, :]).then_inc(xf_stored, 16)
                sp.wait_ge(xf_stored, 16 * v + 16)
                for got, (t0, t1) in zip(spread_in, DMA_STEPS):
                    if not is_first:
                        sp.wait_ge(prod_done, FH * v - (FH - t1))
                    for q in range(2):
                        src = xf_dram[half, FH * q + t0:FH * q + t1, :]
                        sp.dma_start(xspread[H * q:H * q + H, t0 - TS:t1 - TS, :],
                                     src.unsqueeze(0).broadcast_to([H, t1 - t0, POS])).then_inc(got, 16)

            def unit(u, half, is_first, is_last):
                if not is_last:
                    spread(u + 1, 1 - half, False)

            spread(0, 0, True)
            all_units(sp, unit)
            sp.wait_ge(y_done, len(BATCHES))
            sp.dma_start(out.rearrange("b o -> o b"), y[:, :]).then_inc(stored, 16)
            sp.wait_ge(stored, 16)

        @block.gpsimd
        def _(pool):
            nc.gpsimd.memset(xs[:, :, PARTS * FH:], 0.0).then_inc(pad_done, 1)
            pool.wait_ge(ids_in, 16)

            by_unit = lookup[:, :].rearrange("p (u f) -> p u f", f=FH)
            nc.gpsimd.tensor_tensor(rows[:, :, :], by_unit[:, 0:UNITS, :],
                                    by_unit[:, UNITS:, :].broadcast_to([128, UNITS, FH]),
                                    ALU.add).then_inc(rows_done, 1)
            pool.wait_ge(rows_done, 1)
            for u in range(UNITS):
                if u >= 2:
                    pool.wait_ge(split_done, u - 1)
                for f in range(FH):
                    nc.gpsimd.indirect_dma_start(
                        out=emb[:, u % 2, D * f:D * (f + 1)], out_offset=None, in_=a["tables"][:, :],
                        in_offset=bass.IndirectOffsetOnAxis(ap=rows[:, u, f:f + 1], axis=0),
                    ).then_inc(gathered[u % 2], 16)

        @block.tensor
        def _(pe):
            def spread(t, half):
                for c in range(2):
                    last = nc.tensor.matmul(spread_ps[t % 2][:, CHUNK * c:CHUNK * (c + 1)],
                                            sel[:, C_SPREAD + 128 * t:C_SPREAD + 128 * (t + 1)],
                                            xt[:, half, CHUNK * c:CHUNK * (c + 1)], start=True, stop=True)
                last.then_inc(spread_mm, 1)

            def back(w, half, t, beside_front):
                if t == 2:
                    pe.wait_ge(x2_done, w + 1)
                    if beside_front:
                        pe.wait_ge(xf_done, 2 * w + 6)
                    for g in range(CG):
                        last = nc.tensor.transpose(misc[:, 128 * g:128 * (g + 1)], x2[:, 128 * g:128 * (g + 1)], eye_f)
                    last.then_inc(x2t_mm, 1)
                if t == 4:
                    pe.wait_ge(x2t_done, w + 1)
                    if beside_front:
                        pe.wait_ge(sq_done, 6 * w + 14)
                    for c, sums in enumerate((misc, pair_ps)):
                        for g in range(CG):
                            for q in range(2):
                                last = nc.tensor.matmul(
                                    sums[H * q:H * q + H, GF * g:GF * g + (FH + q) * GB], x2t[:, g, H * c:H * c + H],
                                    xdiag[:, half, CG * c + g, FH * q:FH * q + FH + q, :].rearrange("p f b -> p (f b)"),
                                    start=True, stop=True)
                        last.then_inc(gram_mm, 1)

            def join(v, half, behind):
                pe.wait_ge(xf_done, 2 * v + 2)
                if behind:
                    pe.wait_ge(gram_done, 2 * v - 2)
                for g in range(GROUPS):
                    last = nc.tensor.matmul(misc[:, F * g:F * (g + 1)], xt[:, half, 128 * g:128 * (g + 1)],
                                            sel[:, C_JOIN:C_JOIN + F], start=True, stop=True)
                last.then_inc(join_mm, 1)

            def front(v, half, t, is_first, behind):
                if t == 0:
                    for d in range(D):
                        for q in range(2):
                            last = nc.tensor.transpose(misc_bf[64 * q:64 * q + 64, UNIT_B * d:UNIT_B * (d + 1)],
                                                       xs[64 * q:64 * q + 64, d, :],
                                                       sel[64 * q:64 * q + 64, C_EYE:C_EYE + 64])
                    last.then_inc(xt_mm, 1)
                if t == 1:
                    pe.wait_ge(xt_done, v + 1)
                    for c in range(2):
                        last = nc.tensor.matmul(misc[64 * c:64 * c + F, :], sel[:, C_JOIN:C_JOIN + F],
                                                xt[:, half, CHUNK * c:CHUNK * (c + 1)], start=True, stop=True)
                    last.then_inc(xf_mm, 1)
                for i in {1: (0,), 2: (1,), 3: (2, 3), 4: (4, 5)}.get(t, ()):
                    if i == 5 and not is_first:
                        pe.wait_ge(sq_done, 6 * v + 2)
                    k, c = i // 2, i % 2
                    nc.tensor.matmul((first_pairs if is_first else pair_banks)[i][0:PR, :],
                                     sel[:, C_PAIR + PR * k:C_PAIR + PR * (k + 1)],
                                     xt[:, half, CHUNK * c:CHUNK * (c + 1)], start=True, stop=True).then_inc(pair_mm, 1)
                if t == 3 and is_first:
                    join(v, half, behind)
                if t in (3, 5, 6):
                    k = (3, 5, 6).index(t)
                    pe.wait_ge(sq_done, 6 * v + 2 * k + 2)
                    if k == 0 and not is_first:
                        pe.wait_ge(x1_done, 4 * v)
                    for c in range(2):
                        last = nc.tensor.matmul(x1_ps[H * c:H * c + H, :], w0p[:, k, :], sq[:, k, c, :],
                                                start=(k == 0), stop=(k == PT - 1))
                    if k == PT - 1:
                        last.then_inc(x1_mm, 1)
                if t == 6 and not is_first:
                    join(v, half, behind)

            g_all = gram[:, :].rearrange("p (u f b) -> p f u b", f=FH, b=UNIT_B)

            def mlp(n, step):
                u0, un = BATCHES[n]
                cols = slice(UNIT_B * u0, UNIT_B * (u0 + un))
                width = UNIT_B * un
                hidden = [spread_ps[m // 2][:, CHUNK * (m % 2):CHUNK * (m % 2) + width] for m in range(M1)]
                if step == 0:
                    pe.wait_ge(gram_done, 2 * (u0 + un))
                    pe.wait_ge(x1_done, 4 * UNITS)
                    for t in range(0, FH, 2):
                        for s in range(2):
                            last = nc.tensor.matmul(x1_ps[H * s:H * s + H, 0:width], w2[:, t + s, :],
                                                    g_all[:, t + s, u0:u0 + un, :], start=(t == 0), stop=(t == FH - 2))
                    last.then_inc(z3_mm, 1)
                if step == 1:
                    pe.wait_ge(z1_done, u0 + un)
                    for m in range(M1):
                        nc.tensor.matmul(hidden[m], wt1a[:, 128 * m:128 * (m + 1)], z12[:, cols], start=True, stop=False)
                if step == 2:
                    pe.wait_ge(z3_done, n + 1)
                    for m in range(M1):
                        nc.tensor.matmul(hidden[m], wt1b[:, 128 * m:128 * (m + 1)], z3d[:, cols], start=False,
                                         stop=True).then_inc(h1_mm, 1)
                if step == 3:
                    for k in range(M1):
                        pe.wait_ge(h1_done, M1 * n + k + 1)
                        for m in range(M2):
                            last = nc.tensor.matmul((pair_ps, x1_ps)[m][:, 0:width], wt2[:, k, 128 * m:128 * (m + 1)],
                                                    h1[:, k, cols], start=(k == 0), stop=(k == M1 - 1))
                            if k == M1 - 1:
                                last.then_inc(h2_mm, 1)
                if step == 4:
                    if n == 0:
                        pe.wait_ge(gram_done, 2 * (UNITS - 1))
                    for k in range(M2):
                        pe.wait_ge(h2_done, M2 * n + k + 1)
                        last = nc.tensor.matmul(misc[0:1, 0:width], wt3[:, k:k + 1], h2[:, k, cols],
                                                start=(k == 0), stop=(k == M2 - 1))
                    last.then_inc(y_mm, 1)

            def unit(u, half, is_first, is_last):
                late = FIRST_LATE if is_first else 0
                for t in range(FH):
                    if t == late and not is_last:
                        pe.wait_ge(split_done, u + 2)
                        pe.wait_ge(xdiag_done, u + 1)
                    pe.wait_ge(prod_done, FH * u + t + 1)
                    if t + 2 < TS:
                        spread(t + 2, half)
                    if t >= FH - 2 and not is_last:
                        spread(t + 2 - FH, 1 - half)
                    if t == late and not is_last:
                        front(u + 1, 1 - half, 0, False, not is_first)
                    if t == 0 and not is_first:
                        pe.wait_ge(x2_done, u)
                    for c in range(2):
                        last = nc.tensor.matmul(x2_ps[H * c:H * c + H, :], w1[:, t, :],
                                                prod[:, t % RING, CHUNK * c:CHUNK * (c + 1)],
                                                start=(t == 0), stop=(t == FH - 1))
                    last.then_inc(x2_mm, 1)
                    if t > late and not is_last:
                        front(u + 1, 1 - half, t - late, False, not is_first)
                    if not is_first:
                        back(u - 1, 1 - half, t, not is_last)
                    if is_last and t in MLP_STEPS:
                        mlp(0, MLP_STEPS.index(t))

            pe.wait_ge(w0_in, 32)
            for k in range(PT):
                for r in range(W0K):
                    last = nc.tensor.matmul(misc[0:PR, H * k:H * (k + 1)], fold[:, r, PR * k:PR * (k + 1)], w0[:, r, :],
                                            start=(r == 0), stop=(r == W0K - 1))
            last.then_inc(w0p_mm, 1)
            pe.wait_ge(sel_done, 1)
            pe.wait_ge(cf_in, 16)
            pe.wait_ge(ones_done, 2)
            pe.wait_ge(pad_done, 1)
            pe.wait_ge(w0p_done, 1)
            pe.wait_ge(split_done, 1)
            for t in range(7):
                front(0, 0, t, True, False)
            pe.wait_ge(w1_in, 32)
            for t in range(2):
                spread(t, 0)
            pe.wait_ge(w2_in, 32)
            pe.wait_ge(top_in, 16 * 7)
            all_units(pe, unit)
            pe.wait_ge(y_done, 1)
            for t in (2, 4):
                back(UNITS - 1, (UNITS - 1) % 2, t, False)
            for step in range(5):
                mlp(1, step)

        @block.scalar
        def _(act):
            act.dma_start(sel_f32[:, :], a["const_sel"][:, :]).then_inc(sel_in, 16)
            for dst, src in ((wt1a[:, :], a["W_top1"][0:128, :]), (wt1b[:, :], a["W_top1"][128:, :]),
                             (wt2[:, :, :], a["W_top2"].rearrange("(k p) n -> p k n", p=128)), (wt3[:, :], a["W_top3"][:, :]),
                             (b1[:, :], a["b_top1"][:, :]), (b2[:, :], a["b_top2"][:, :]), (z3d[H:, :], a["dense_t"][:, :])):
                act.dma_start(dst, src).then_inc(top_in, 16)

            def copy(o, i):
                return nc.scalar.activation(o, i, ACT.Copy)

            def x2_copy(w):
                act.wait_ge(x2_mm, FH * (w + 1))
                copy(x2[:, :], x2_ps[:, :]).then_inc(x2_done, 1)

            def back(w, t):
                if t == 2:
                    act.wait_ge(x2t_mm, w + 1)
                    copy(x2t[:, :, :].rearrange("p g m -> p (g m)"), misc[:, :]).then_inc(x2t_done, 1)
                if t == 4:
                    for c, bank in enumerate((misc, pair_ps)):
                        act.wait_ge(gram_mm, 2 * w + c + 1)
                        sums = bank[:, 0:CG * GF].rearrange("p (g f b) -> p g f b", g=CG, b=GB)
                        here = gram[:, bass.ds(w * (FH * UNIT_B), FH * UNIT_B)]
                        here = here.rearrange("p (f c g b) -> p c g f b", f=FH, c=2, g=CG)
                        copy(here[:, c], sums[:, :, 0:FH, :])
                        zs = z12[H:2 * H, bass.ds(w * UNIT_B + c * CG * GB, CG * GB)]
                        copy(zs.rearrange("p (g b) -> p g b", g=CG), sums[H:2 * H, :, FH, :]).then_inc(gram_done, 1)

            def front(v, half, t, is_first):
                if t == 0:
                    act.wait_ge(xt_mm, v + 1)
                    copy(xt[:, half, :].rearrange("p (g d b) -> p g d b", g=GROUPS, d=D),
                         misc_bf.rearrange("p (d g b) -> p g d b", d=D, g=GROUPS)).then_inc(xt_done, 1)
                if t == 1 and not is_first:
                    act.wait_ge(xf_stored, 16 * v)
                    act.wait_ge(xf_mm, v + 1)
                    for c in range(2):
                        copy(xf[:, CHUNK * c:CHUNK * (c + 1)], misc[64 * c:64 * c + F, :]).then_inc(xf_done, 1)
                for i in {1: (0,), 2: (1,), 3: (2, 3), 4: (4, 5)}.get(t, ()):
                    if i == 0 and not is_first:
                        act.wait_ge(x1_mm, v)
                    act.wait_ge(pair_mm, 6 * v + i + 1)
                    nc.scalar.activation(sq[:, i // 2, i % 2, :], (first_pairs if is_first else pair_banks)[i][0:PR, :],
                                         ACT.Square).then_inc(sq_done, 1)
                if t == 6:
                    act.wait_ge(x1_mm, v + 1)
                    for c in range(1 if is_first else 2):
                        for q in range(2):
                            copy(x1[H * q:H * q + H, half, CHUNK * c:CHUNK * (c + 1)],
                                 x1_ps[H * c:H * c + H, :]).then_inc(x1_done, 1)

            def mlp(n, step):
                u0, un = BATCHES[n]
                cols = slice(UNIT_B * u0, UNIT_B * (u0 + un))
                width = UNIT_B * un
                if step == 0:
                    act.wait_ge(z3_mm, n + 1)
                    copy(z3d[0:H, cols], x1_ps[H:2 * H, 0:width]).then_inc(z3_half, 1)
                if step == 2:
                    for m in range(M1):
                        act.wait_ge(h1_mm, M1 * n + m + 1)
                        hidden = spread_ps[m // 2][:, CHUNK * (m % 2):CHUNK * (m % 2) + width]
                        nc.scalar.activation(h1[:, m, cols], hidden, ACT.Relu, bias=b1[:, m:m + 1]).then_inc(h1_done, 1)
                if step == 3:
                    for m in range(M2):
                        act.wait_ge(h2_mm, M2 * n + m + 1)
                        nc.scalar.activation(h2[:, m, cols], (pair_ps, x1_ps)[m][:, 0:width], ACT.Relu,
                                             bias=b2[:, m:m + 1]).then_inc(h2_done, 1)
                if step == 4:
                    act.wait_ge(y_mm, n + 1)
                    copy(y[:, cols], misc[0:1, 0:width]).then_inc(y_done, 1)

            def unit(u, half, is_first, is_last):
                late = FIRST_LATE if is_first else 0
                if not is_first:
                    x2_copy(u - 1)
                for t in range(FH):
                    if t >= late and not is_last:
                        front(u + 1, 1 - half, t - late, False)
                    if not is_first:
                        back(u - 1, t)
                    if is_last and t in MLP_STEPS:
                        mlp(0, MLP_STEPS.index(t))

            act.wait_ge(w0p_mm, 1)
            copy(w0p[:, :, :].rearrange("p k o -> p (k o)"), misc[0:PR, 0:PT * H]).then_inc(w0p_done, 1)
            for t in range(7):
                front(0, 0, t, True)
            act.wait_ge(top_in, 16 * 7)
            all_units(act, unit)
            x2_copy(UNITS - 1)
            for t in (2, 4):
                back(UNITS - 1, t)
            for step in (0, 2, 3, 4):
                mlp(1, step)

        @block.vector
        def _(dve):
            def split(v, half, step):
                parts = xs[:, :, 0:PARTS * FH].rearrange("p d (s f) -> p s f d", s=PARTS)
                x = emb[:, half, :].rearrange("p (f d) -> p f d", d=D)
                r = rest[:, :].rearrange("p (f d) -> p f d", d=D)
                if step == 0:
                    dve.wait_ge(gathered[half], 8 * FH * (v - half) + 16 * FH)
                    nc.vector.tensor_copy(parts[:, 0], x).then_inc(split_step, 1)
                if step == 1:
                    dve.wait_ge(split_step, 3 * v + 1)
                    nc.vector.tensor_tensor(r, x, parts[:, 0], ALU.subtract).then_inc(split_step, 1)
                if step == 2:
                    dve.wait_ge(split_step, 3 * v + 2)
                    nc.vector.tensor_copy(parts[:, 1], r).then_inc(split_step, 1)
                if step == 3:
                    dve.wait_ge(split_step, 3 * v + 3)
                    nc.vector.tensor_tensor(parts[:, 2], r, parts[:, 1], ALU.subtract).then_inc(split_done, 1)

            def diagonal(v, half):
                dve.wait_ge(join_mm, v + 1)
                shape = [128, GROUPS, F, GB]
                x = misc[:, 0:GROUPS * F].rearrange("p (g f) -> p g f", g=GROUPS)
                nc.vector.tensor_tensor(xdiag[:, half, :, 0:F, :], x.unsqueeze(3).broadcast_to(shape),
                                        block_mask.unsqueeze(1).unsqueeze(1).broadcast_to(shape),
                                        ALU.mult).then_inc(xdiag_done, 1)

            def sum_x1(u, half):
                here = z12[0:H, bass.ds(u * UNIT_B, UNIT_B)].rearrange("p (g b) -> p g b", g=GROUPS)
                nc.vector.tensor_reduce(here, x1[0:H, half, :].rearrange("p (g d b) -> p g b d", g=GROUPS, d=D),
                                        AX.X, ALU.add).then_inc(z1_done, 1)

            def product(u, half, t, is_first):
                if t == 0:
                    dve.wait_ge(x1_done, 4 * u + 4)
                if t < TS:
                    dve.wait_ge(spread_mm, TS * u + t + 1)
                    x = spread_ps[t % 2][:, :]
                else:
                    got = [t0 <= t < t1 for t0, t1 in DMA_STEPS].index(True)
                    dve.wait_ge(spread_in[got], 32 * u + 32)
                    x = xspread[:, t - TS, :]
                if t >= RING or not is_first:
                    dve.wait_ge(x2_mm, FH * u + t - RING + 1)
                nc.vector.tensor_tensor(prod[:, t % RING, :], x, x1[:, half, :], ALU.mult).then_inc(prod_done, 1)

            def unit(u, half, is_first, is_last):
                late = FIRST_LATE if is_first else 0
                for t in range(FH):
                    if t == late and not is_last:
                        for s in range(4):
                            split(u + 1, 1 - half, s)
                    product(u, half, t, is_first)
                    if t == 2:
                        sum_x1(u, half)
                    if is_last and t == MLP_STEPS[0] + 2:
                        sum_z3(0)
                    if t == DIAGONAL_STEP + is_first and not is_last:
                        diagonal(u + 1, 1 - half)

            def sum_z3(n):
                u0, un = BATCHES[n]
                cols = slice(UNIT_B * u0, UNIT_B * (u0 + un))
                dve.wait_ge(z3_half, n + 1)
                nc.vector.tensor_tensor(z3d[0:H, cols], x1_ps[0:H, 0:UNIT_B * un], z3d[0:H, cols],
                                        ALU.add).then_inc(z3_done, 1)

            dve.wait_ge(sel_in, 16)
            nc.vector.tensor_copy(sel[:, :], sel_f32[:, :]).then_inc(sel_done, 1)
            dve.wait_ge(cf_in, 16)
            for p in range(2):
                nc.vector.tensor_copy(xdiag[:, p, :, F, :],
                                      block_mask.unsqueeze(1).broadcast_to([128, GROUPS, GB])).then_inc(ones_done, 1)
            for s in range(4):
                split(0, 0, s)
            dve.wait_ge(xf_mm, 1)
            for c in range(2):
                nc.vector.tensor_copy(xf[:, CHUNK * c:CHUNK * (c + 1)], misc[64 * c:64 * c + F, :]).then_inc(xf_done, 1)
            diagonal(0, 0)
            dve.wait_ge(x1_mm, 1)
            for q in range(2):
                nc.vector.tensor_copy(x1[H * q:H * q + H, 0, CHUNK:], x1_ps[H:2 * H, :]).then_inc(x1_done, 1)
            all_units(dve, unit)
            sum_z3(1)


DIAGONAL_STEP = 10
MLP_STEPS = (7, 8, 9, 10, 11)


def constants():
    pairs = [(i, j) for i in range(F) for j in range(i, F)]
    fold = np.zeros((F * F, PAIRS), np.float32)
    add = np.zeros((F, PAIRS), np.float32)
    for m, (i, j) in enumerate(pairs):
        add[i, m] = add[j, m] = 1
        if i != j:
            fold[i * F + j, m] = fold[j * F + i, m] = 0.5
        else:
            fold[i * F:(i + 1) * F, m] = -0.5
            fold[i::F, m] = -0.5
            fold[i * F + i, m] = 1
    spread = np.zeros((F, TS, 128), np.float32)
    for t in range(TS):
        spread[t, t, 0:H] = spread[t + FH, t, H:] = 1
    by_feature = np.concatenate([add, spread.reshape(F, -1), np.eye(F, dtype=np.float32)], axis=1)
    sel = np.zeros((128, C_SEL), np.float32)
    for q in range(2):
        sel[64 * q:64 * q + PARTS * FH, 0:C_EYE] = np.tile(by_feature[FH * q:FH * q + FH], (PARTS, 1))
        sel[64 * q:64 * q + 64, C_EYE:] = np.eye(64)
    const_f32 = np.zeros((128, C_F32), np.float32)
    const_f32[:, 0:128] = np.eye(128)
    const_f32[:, 128:] = np.tile(np.eye(GB), (D, 1))
    return fold, sel, const_f32


def kernel(**inputs):
    import concourse.bacc as bacc
    from concourse.bass_utils import run_bass_kernel_spmd as run

    nc = bacc.Bacc("TRN2", target_bir_lowering=False, num_devices=1)
    arrays = {n: np.ascontiguousarray(x) for n, x in inputs.items()}
    arrays["dense_t"] = np.ascontiguousarray(arrays.pop("dense_ctx").T)
    tables = [arrays.pop(f"tbl_{f}") for f in range(F)]
    first = np.cumsum([0] + [t.shape[0] for t in tables[:-1]]).astype(np.int32)
    arrays["tables"] = np.concatenate(tables, axis=0)
    ids = arrays.pop("ids").reshape(UNITS, UNIT_B, 2, FH).transpose(2, 1, 0, 3).reshape(128, UNITS * FH)
    arrays["lookup"] = np.concatenate([ids, np.repeat(first.reshape(2, FH), UNIT_B, axis=0)], axis=1)
    for name in ("W_top3", "b_top1", "b_top2"):
        arrays[name] = np.ascontiguousarray(arrays[name].reshape(-1, 128).T)
    arrays["const_fold"], arrays["const_sel"], arrays["const_f32"] = constants()
    args = {n: nc.dram_tensor(n, x.shape, mybir.dt.from_np(x.dtype), kind="ExternalInput").ap()
            for n, x in arrays.items()}
    out = nc.dram_tensor("out", (B, 1), F32, kind="ExternalOutput").ap()
    dlrm_tower(nc, args, out)
    r = run(nc, [arrays], core_ids=[0])
    return r.results[0]["out"]
```

```python
import concourse.bass as bass
from concourse import mybir
from contextlib import ExitStack

import numpy as np

F32 = mybir.dt.float32
BF16 = mybir.dt.bfloat16
I32 = mybir.dt.int32
ALU = mybir.AluOpType
ACT = mybir.ActivationFunctionType
AX = mybir.AxisListType

B, F, D, H = 512, 24, 16, 64
PARTS = 3
UNIT_B = 64
UNITS = B // UNIT_B
GB = 8
GROUPS = UNIT_B // GB
CG = GROUPS // 2
CHUNK = CG * GB * D
POS = 2 * CHUNK
FH = F // 2
TS = 3
DMA_STEPS = ((3, 5), (5, 8), (8, 12))
PAIRS = F * (F + 1) // 2
PT = 3
PR = PAIRS // PT
W0K = 6
W0R = F * F // W0K
GF = (FH + 1) * GB
RING = 6
FOLD_AFTER = 9
FIRST_LATE = 2
D_CTX, N1, N2 = 16, 512, 256
M1, M2 = N1 // 128, N2 // 128
C_PAIR, C_SPREAD = 0, PAIRS
C_JOIN = C_SPREAD + TS * 128
C_EYE = C_JOIN + F
C_SEL = C_EYE + 64
C_F32 = 128 + GB
BATCHES = ((0, 6), (6, 2))
PAIR_STEPS = {1: (0,), 2: (1,), 3: (2, 3), 4: (4, 5)}
CONTRACT_STEPS = (3, 5, 6)
FRONT_STEPS = 7
TURN_STEP, GRAM_STEP = 2, 4
SUM3, TOP1_A, TOP1_B, TOP2, TOP3 = 0, 1, 2, 3, 3 + M1
SUM_X1_STEP = 6
DIAGONAL_STEP = 11
MLP_STEPS = {7: (SUM3,), 8: (TOP1_A,), 9: (TOP1_B,), 10: (TOP2, TOP2 + 1)}
SUM_Z3_STEP = 9


def dlrm_tower(nc, a, out):
    ctx = ExitStack()
    with ctx:
        def sb(name, shape, dt=F32):
            return ctx.enter_context(nc.sbuf_tensor(name, shape, dt))

        def ps(name, cols=512):
            return ctx.enter_context(nc.psum_tensor(name, [128, cols], F32))

        def sem(name):
            return ctx.enter_context(nc.semaphore(name))

        lookup = sb("lookup_sb", [128, (UNITS + 1) * FH], I32)
        rows = sb("rows", [128, UNITS, FH], I32)
        sel_f32 = sb("sel_f32", [128, C_SEL])
        sel = sb("sel", [128, C_SEL], BF16)
        cf = sb("cf", [128, C_F32])
        fold = sb("fold", [W0R, W0K, PAIRS])
        w0 = sb("w0", [W0R, W0K, H])
        w0p = sb("w0p", [PR, PT, H])
        w1 = sb("w1", [128, FH, H])
        w2 = sb("w2", [128, FH, H])
        wt1a = sb("wt1a", [128, N1])
        wt1b = sb("wt1b", [H + D_CTX, N1])
        wt2 = sb("wt2", [128, M1, N2])
        wt3 = sb("wt3", [128, M2])
        b1 = sb("b1", [128, M1])
        b2 = sb("b2", [128, M2])
        emb = sb("emb", [128, 2, FH * D])
        rest = sb("rest", [128, FH * D])
        xs = sb("xs", [128, D, 64], BF16)
        xt = sb("xt", [128, 2, POS], BF16)
        xf = sb("xf", [F, POS])
        xf_dram = nc.dram_tensor("xf_dram", (2, F, POS), F32, kind="Internal").ap()
        xspread = sb("xspread", [128, FH - TS, POS])
        xdiag = sb("xdiag", [128, 2, GROUPS, F + 1, GB])
        sq = sb("sq", [PR, PT, 2, CHUNK])
        x1 = sb("x1", [128, 2, POS])
        prod = sb("prod", [128, RING, POS])
        x2 = sb("x2", [128, CHUNK])
        x2t = sb("x2t", [128, CG, 128])
        gram = sb("gram", [128, UNITS * FH * UNIT_B])
        z12 = sb("z12", [128, B])
        z3d = sb("z3d", [H + D_CTX, B])
        h1 = sb("h1", [128, M1, B])
        h2 = sb("h2", [128, M2, B])
        y = sb("y", [1, B])

        spread_ps = [ps(f"spread{i}", POS) for i in range(2)]
        x2_ps, x1_ps, pair_ps, misc = ps("x2_ps"), ps("x1_ps"), ps("pair_ps"), ps("misc")
        misc_bf = misc[:, :].bitcast(BF16)

        ids_in, rows_done, sel_in, sel_done, cf_in = (sem(n) for n in (
            "ids_in", "rows_done", "sel_in", "sel_done", "cf_in"))
        w0_in, w1_in, w2_in, top_in, pad_done, ones_done = (sem(n) for n in (
            "w0_in", "w1_in", "w2_in", "top_in", "pad_done", "ones_done"))
        gathered = [sem("gathered_even"), sem("gathered_odd")]
        split_step, split_done = sem("split_step"), sem("split_done")
        w0p_mm, w0p_done = sem("w0p_mm"), sem("w0p_done")
        xt_mm, xt_done = sem("xt_mm"), sem("xt_done")
        xf_mm, xf_done, xf_stored = sem("xf_mm"), sem("xf_done"), sem("xf_stored")
        spread_in = [sem(f"spread_in{i}") for i in range(len(DMA_STEPS))]
        join_mm, xdiag_done = sem("join_mm"), sem("xdiag_done")
        pair_mm, sq_done = sem("pair_mm"), sem("sq_done")
        x1_mm, x1_done, z1_done = sem("x1_mm"), sem("x1_done"), sem("z1_done")
        spread_mm, prod_done, x2_mm, x2_done = sem("spread_mm"), sem("prod_done"), sem("x2_mm"), sem("x2_done")
        x2t_mm, x2t_done = sem("x2t_mm"), sem("x2t_done")
        gram_mm, gram_done = sem("gram_mm"), sem("gram_done")
        z3_mm, z3_half, z3_done, h1_mm, h1_done = (sem(n) for n in ("z3_mm", "z3_half", "z3_done", "h1_mm", "h1_done"))
        h2_mm, h2_done, y_mm, y_done, stored = (sem(n) for n in ("h2_mm", "h2_done", "y_mm", "y_done", "stored"))

        eye_f = cf[:, 0:128]
        block_mask = cf[:, 128:128 + GB]
        spread_halves = [s[:, CHUNK * c:CHUNK * (c + 1)] for s in spread_ps for c in range(2)]
        pair_banks = [pair_ps[:, :]] + [spread_halves[i] for i in (2, 3, 0, 1, 2)]
        first_pairs = [pair_ps[:, :], x2_ps[:, :]] + spread_halves
        h2_banks = (spread_halves[0:M2], (pair_ps, x1_ps))
        y_banks = (spread_halves[2], misc)

        block = ctx.enter_context(nc.Block())

        def all_units(engine, unit):
            unit(0, 0, True, False)
            with engine.Fori(0, (UNITS - 2) // 2) as i:
                for s in range(2):
                    unit(2 * i + 1 + s, 1 - s, False, False)
            unit(UNITS - 1, 1, False, True)

        @block.sync
        def _(sp):
            sp.dma_start(lookup[:, :], a["lookup"][:, :]).then_inc(ids_in, 16)
            sp.dma_start(fold[:, :, :], a["const_fold"].rearrange("(k p) n -> p k n", p=W0R)).then_inc(w0_in, 16)
            sp.dma_start(w0[:, :, :], a["L0_rec_W0"].rearrange("(k p) o -> p k o", p=W0R)).then_inc(w0_in, 16)
            sp.dma_start(cf[:, :], a["const_f32"][:, :]).then_inc(cf_in, 16)
            for w, name, got in ((w1, "L0_rec_W1", w1_in), (w2, "L0_rec_W2", w2_in)):
                by_step = a[name].rearrange("(q t h) o -> q h t o", q=2, t=FH)
                for q in range(2):
                    sp.dma_start(w[H * q:H * q + H, :, :], by_step[q]).then_inc(got, 16)

            def spread(v, half, is_first):
                sp.wait_ge(xf_done, 2 * v + 2)
                sp.dma_start(xf_dram[half], xf[:, :]).then_inc(xf_stored, 16)
                sp.wait_ge(xf_stored, 16 * v + 16)
                for got, (t0, t1) in zip(spread_in, DMA_STEPS):
                    if not is_first:
                        sp.wait_ge(prod_done, FH * v - (FH - t1))
                    for q in range(2):
                        src = xf_dram[half, FH * q + t0:FH * q + t1, :]
                        sp.dma_start(xspread[H * q:H * q + H, t0 - TS:t1 - TS, :],
                                     src.unsqueeze(0).broadcast_to([H, t1 - t0, POS])).then_inc(got, 16)

            def unit(u, half, is_first, is_last):
                if not is_last:
                    spread(u + 1, 1 - half, False)

            spread(0, 0, True)
            all_units(sp, unit)
            sp.wait_ge(y_done, len(BATCHES))
            sp.dma_start(out.rearrange("b o -> o b"), y[:, :]).then_inc(stored, 16)
            sp.wait_ge(stored, 16)

        @block.gpsimd
        def _(pool):
            pool.wait_ge(ids_in, 16)

            by_unit = lookup[:, :].rearrange("p (u f) -> p u f", f=FH)
            nc.gpsimd.tensor_tensor(rows[:, :, :], by_unit[:, 0:UNITS, :],
                                    by_unit[:, UNITS:, :].broadcast_to([128, UNITS, FH]),
                                    ALU.add).then_inc(rows_done, 1)
            pool.wait_ge(rows_done, 1)
            for u in range(UNITS):
                if u >= 2:
                    pool.wait_ge(split_done, u - 1)
                for f in range(FH):
                    if u == 0 and f == FOLD_AFTER:
                        nc.gpsimd.memset(xs[:, :, PARTS * FH:], 0.0).then_inc(pad_done, 1)
                    nc.gpsimd.indirect_dma_start(
                        out=emb[:, u % 2, D * f:D * (f + 1)], out_offset=None, in_=a["tables"][:, :],
                        in_offset=bass.IndirectOffsetOnAxis(ap=rows[:, u, f:f + 1], axis=0),
                    ).then_inc(gathered[u % 2], 16)

        @block.tensor
        def _(pe):
            def spread(t, half):
                for c in range(2):
                    last = nc.tensor.matmul(spread_ps[t % 2][:, CHUNK * c:CHUNK * (c + 1)],
                                            sel[:, C_SPREAD + 128 * t:C_SPREAD + 128 * (t + 1)],
                                            xt[:, half, CHUNK * c:CHUNK * (c + 1)], start=True, stop=True)
                last.then_inc(spread_mm, 1)

            def back(w, half, t, beside_front):
                if t == TURN_STEP:
                    pe.wait_ge(x2_done, w + 1)
                    if beside_front:
                        pe.wait_ge(xf_done, 2 * w + 6)
                    for g in range(CG):
                        last = nc.tensor.transpose(misc[:, 128 * g:128 * (g + 1)], x2[:, 128 * g:128 * (g + 1)], eye_f)
                    last.then_inc(x2t_mm, 1)
                if t == GRAM_STEP:
                    pe.wait_ge(x2t_done, w + 1)
                    if beside_front:
                        pe.wait_ge(sq_done, 6 * w + 14)
                    for c, sums in enumerate((misc, pair_ps)):
                        for g in range(CG):
                            for q in range(2):
                                last = nc.tensor.matmul(
                                    sums[H * q:H * q + H, GF * g:GF * g + (FH + q) * GB], x2t[:, g, H * c:H * c + H],
                                    xdiag[:, half, CG * c + g, FH * q:FH * q + FH + q, :].rearrange("p f b -> p (f b)"),
                                    start=True, stop=True)
                        last.then_inc(gram_mm, 1)

            def join(v, half, behind):
                pe.wait_ge(xf_done, 2 * v + 2)
                if behind:
                    pe.wait_ge(gram_done, 2 * v - 2)
                for g in range(GROUPS):
                    last = nc.tensor.matmul(misc[:, F * g:F * (g + 1)], xt[:, half, 128 * g:128 * (g + 1)],
                                            sel[:, C_JOIN:C_JOIN + F], start=True, stop=True)
                last.then_inc(join_mm, 1)

            def front(v, half, t, is_first, behind):
                if t == 0:
                    for d in range(D):
                        for q in range(2):
                            last = nc.tensor.transpose(misc_bf[64 * q:64 * q + 64, UNIT_B * d:UNIT_B * (d + 1)],
                                                       xs[64 * q:64 * q + 64, d, :],
                                                       sel[64 * q:64 * q + 64, C_EYE:C_EYE + 64])
                    last.then_inc(xt_mm, 1)
                if t == 1:
                    pe.wait_ge(xt_done, v + 1)
                    for c in range(2):
                        last = nc.tensor.matmul(misc[64 * c:64 * c + F, :], sel[:, C_JOIN:C_JOIN + F],
                                                xt[:, half, CHUNK * c:CHUNK * (c + 1)], start=True, stop=True)
                    last.then_inc(xf_mm, 1)
                for i in PAIR_STEPS.get(t, ()):
                    if i == 5 and not is_first:
                        pe.wait_ge(sq_done, 6 * v + 2)
                    k, c = i // 2, i % 2
                    nc.tensor.matmul((first_pairs if is_first else pair_banks)[i][0:PR, :],
                                     sel[:, C_PAIR + PR * k:C_PAIR + PR * (k + 1)],
                                     xt[:, half, CHUNK * c:CHUNK * (c + 1)], start=True, stop=True).then_inc(pair_mm, 1)
                if t == 3 and is_first:
                    join(v, half, behind)
                if t in CONTRACT_STEPS:
                    k = CONTRACT_STEPS.index(t)
                    pe.wait_ge(sq_done, 6 * v + 2 * k + 2)
                    if k == 0 and not is_first:
                        pe.wait_ge(x1_done, 4 * v)
                    for c in range(2):
                        last = nc.tensor.matmul(x1_ps[H * c:H * c + H, :], w0p[:, k, :], sq[:, k, c, :],
                                                start=(k == 0), stop=(k == PT - 1))
                    if k == PT - 1:
                        last.then_inc(x1_mm, 1)
                if t == CONTRACT_STEPS[-1] and not is_first:
                    join(v, half, behind)

            g_all = gram[:, :].rearrange("p (u f b) -> p f u b", f=FH, b=UNIT_B)

            def mlp(n, step):
                u0, un = BATCHES[n]
                cols = slice(UNIT_B * u0, UNIT_B * (u0 + un))
                width = UNIT_B * un
                hidden = [bank[:, 0:width] for bank in spread_halves]
                if step == SUM3:
                    pe.wait_ge(gram_done, 2 * (u0 + un))
                    pe.wait_ge(x1_done, 4 * UNITS)
                    for t in range(0, FH, 2):
                        for s in range(2):
                            last = nc.tensor.matmul(x1_ps[H * s:H * s + H, 0:width], w2[:, t + s, :],
                                                    g_all[:, t + s, u0:u0 + un, :], start=(t == 0), stop=(t == FH - 2))
                    last.then_inc(z3_mm, 1)
                if step == TOP1_A:
                    pe.wait_ge(z1_done, u0 + un)
                    if n == 1:
                        pe.wait_ge(y_done, 1)
                    for m in range(M1):
                        nc.tensor.matmul(hidden[m], wt1a[:, 128 * m:128 * (m + 1)], z12[:, cols], start=True, stop=False)
                if step == TOP1_B:
                    pe.wait_ge(z3_done, n + 1)
                    for m in range(M1):
                        nc.tensor.matmul(hidden[m], wt1b[:, 128 * m:128 * (m + 1)], z3d[:, cols], start=False,
                                         stop=True).then_inc(h1_mm, 1)
                if TOP2 <= step < TOP3:
                    k = step - TOP2
                    pe.wait_ge(h1_done, M1 * n + (max(k + 1, M2) if n == 0 else k + 1))
                    for m in range(M2):
                        last = nc.tensor.matmul(h2_banks[n][m][:, 0:width], wt2[:, k, 128 * m:128 * (m + 1)],
                                                h1[:, k, cols], start=(k == 0), stop=(k == M1 - 1))
                        if k == M1 - 1:
                            last.then_inc(h2_mm, 1)
                if step == TOP3:
                    for k in range(M2):
                        pe.wait_ge(h2_done, M2 * n + k + 1)
                        last = nc.tensor.matmul(y_banks[n][0:1, 0:width], wt3[:, k:k + 1], h2[:, k, cols],
                                                start=(k == 0), stop=(k == M2 - 1))
                    last.then_inc(y_mm, 1)

            def unit(u, half, is_first, is_last):
                late = FIRST_LATE if is_first else 0
                for t in range(FH):
                    if t == late and not is_last:
                        pe.wait_ge(split_done, u + 2)
                        pe.wait_ge(xdiag_done, u + 1)
                        if is_first:
                            front(u + 1, 1 - half, 0, False, False)
                    pe.wait_ge(prod_done, FH * u + t + 1)
                    if t + 2 < TS:
                        spread(t + 2, half)
                    if t >= FH - 2 and not is_last:
                        spread(t + 2 - FH, 1 - half)
                    if t == late and not is_last and not is_first:
                        front(u + 1, 1 - half, 0, False, True)
                    if t == 0 and not is_first:
                        pe.wait_ge(x2_done, u)
                    for c in range(2):
                        last = nc.tensor.matmul(x2_ps[H * c:H * c + H, :], w1[:, t, :],
                                                prod[:, t % RING, CHUNK * c:CHUNK * (c + 1)],
                                                start=(t == 0), stop=(t == FH - 1))
                    last.then_inc(x2_mm, 1)
                    if t > late and not is_last:
                        front(u + 1, 1 - half, t - late, False, not is_first)
                    if not is_first:
                        back(u - 1, 1 - half, t, not is_last)
                    if is_last:
                        for step in MLP_STEPS.get(t, ()):
                            mlp(0, step)

            pe.wait_ge(pad_done, 1)
            pe.wait_ge(w0_in, 32)
            for k in range(PT):
                for r in range(W0K):
                    last = nc.tensor.matmul(misc[0:PR, H * k:H * (k + 1)], fold[:, r, PR * k:PR * (k + 1)], w0[:, r, :],
                                            start=(r == 0), stop=(r == W0K - 1))
            last.then_inc(w0p_mm, 1)
            pe.wait_ge(sel_done, 1)
            pe.wait_ge(cf_in, 16)
            pe.wait_ge(ones_done, 2)
            pe.wait_ge(w0p_done, 1)
            pe.wait_ge(split_done, 1)
            for t in range(FRONT_STEPS):
                front(0, 0, t, True, False)
            pe.wait_ge(w1_in, 32)
            for t in range(2):
                spread(t, 0)
            pe.wait_ge(w2_in, 32)
            pe.wait_ge(top_in, 16 * 7)
            all_units(pe, unit)
            mlp(0, TOP2 + 2)
            back(UNITS - 1, (UNITS - 1) % 2, TURN_STEP, False)
            mlp(0, TOP2 + 3)
            back(UNITS - 1, (UNITS - 1) % 2, GRAM_STEP, False)
            mlp(0, TOP3)
            for step in range(TOP3 + 1):
                mlp(1, step)

        @block.scalar
        def _(act):
            act.dma_start(sel_f32[:, :], a["const_sel"][:, :]).then_inc(sel_in, 16)
            for dst, src in ((wt1a[:, :], a["W_top1"][0:128, :]), (wt1b[:, :], a["W_top1"][128:, :]),
                             (wt2[:, :, :], a["W_top2"].rearrange("(k p) n -> p k n", p=128)), (wt3[:, :], a["W_top3"][:, :]),
                             (b1[:, :], a["b_top1"][:, :]), (b2[:, :], a["b_top2"][:, :]), (z3d[H:, :], a["dense_t"][:, :])):
                act.dma_start(dst, src).then_inc(top_in, 16)

            def copy(o, i):
                return nc.scalar.activation(o, i, ACT.Copy)

            def x2_copy(w):
                act.wait_ge(x2_mm, FH * (w + 1))
                copy(x2[:, :], x2_ps[:, :]).then_inc(x2_done, 1)

            def back(w, t):
                if t == TURN_STEP:
                    act.wait_ge(x2t_mm, w + 1)
                    copy(x2t[:, :, :].rearrange("p g m -> p (g m)"), misc[:, :]).then_inc(x2t_done, 1)
                if t == GRAM_STEP:
                    for c, bank in enumerate((misc, pair_ps)):
                        act.wait_ge(gram_mm, 2 * w + c + 1)
                        sums = bank[:, 0:CG * GF].rearrange("p (g f b) -> p g f b", g=CG, b=GB)
                        here = gram[:, bass.ds(w * (FH * UNIT_B), FH * UNIT_B)]
                        here = here.rearrange("p (f c g b) -> p c g f b", f=FH, c=2, g=CG)
                        copy(here[:, c], sums[:, :, 0:FH, :])
                        zs = z12[H:2 * H, bass.ds(w * UNIT_B + c * CG * GB, CG * GB)]
                        copy(zs.rearrange("p (g b) -> p g b", g=CG), sums[H:2 * H, :, FH, :]).then_inc(gram_done, 1)

            def front(v, half, t, is_first):
                if t == 0:
                    act.wait_ge(xt_mm, v + 1)
                    copy(xt[:, half, :].rearrange("p (g d b) -> p g d b", g=GROUPS, d=D),
                         misc_bf.rearrange("p (d g b) -> p g d b", d=D, g=GROUPS)).then_inc(xt_done, 1)
                if t == 1 and not is_first:
                    act.wait_ge(xf_stored, 16 * v)
                    act.wait_ge(xf_mm, v + 1)
                    for c in range(2):
                        copy(xf[:, CHUNK * c:CHUNK * (c + 1)], misc[64 * c:64 * c + F, :]).then_inc(xf_done, 1)
                for i in PAIR_STEPS.get(t, ()):
                    if i == 0 and not is_first:
                        act.wait_ge(x1_mm, v)
                    act.wait_ge(pair_mm, 6 * v + i + 1)
                    nc.scalar.activation(sq[:, i // 2, i % 2, :], (first_pairs if is_first else pair_banks)[i][0:PR, :],
                                         ACT.Square).then_inc(sq_done, 1)
                if t == CONTRACT_STEPS[-1]:
                    act.wait_ge(x1_mm, v + 1)
                    for c in range(1 if is_first else 2):
                        for q in range(2):
                            copy(x1[H * q:H * q + H, half, CHUNK * c:CHUNK * (c + 1)],
                                 x1_ps[H * c:H * c + H, :]).then_inc(x1_done, 1)

            def mlp(n, step):
                u0, un = BATCHES[n]
                cols = slice(UNIT_B * u0, UNIT_B * (u0 + un))
                width = UNIT_B * un
                if step == SUM3:
                    act.wait_ge(z3_mm, n + 1)
                    copy(z3d[0:H, cols], x1_ps[H:2 * H, 0:width]).then_inc(z3_half, 1)
                if step == TOP1_B:
                    for m in range(M1):
                        act.wait_ge(h1_mm, M1 * n + m + 1)
                        nc.scalar.activation(h1[:, m, cols], spread_halves[m][:, 0:width], ACT.Relu,
                                             bias=b1[:, m:m + 1]).then_inc(h1_done, 1)
                if step == TOP3 - 1:
                    for m in range(M2):
                        act.wait_ge(h2_mm, M2 * n + m + 1)
                        nc.scalar.activation(h2[:, m, cols], h2_banks[n][m][:, 0:width], ACT.Relu,
                                             bias=b2[:, m:m + 1]).then_inc(h2_done, 1)
                if step == TOP3:
                    act.wait_ge(y_mm, n + 1)
                    copy(y[:, cols], y_banks[n][0:1, 0:width]).then_inc(y_done, 1)

            def unit(u, half, is_first, is_last):
                late = FIRST_LATE if is_first else 0
                if not is_first:
                    x2_copy(u - 1)
                for t in range(FH):
                    if t >= late and not is_last:
                        front(u + 1, 1 - half, t - late, False)
                    if not is_first:
                        back(u - 1, t)
                    if is_last:
                        for step in MLP_STEPS.get(t, ()):
                            mlp(0, step)

            act.wait_ge(w0p_mm, 1)
            copy(w0p[:, :, :].rearrange("p k o -> p (k o)"), misc[0:PR, 0:PT * H]).then_inc(w0p_done, 1)
            for t in range(FRONT_STEPS):
                front(0, 0, t, True)
            act.wait_ge(top_in, 16 * 7)
            all_units(act, unit)
            x2_copy(UNITS - 1)
            back(UNITS - 1, TURN_STEP)
            mlp(0, TOP2 + 3)
            back(UNITS - 1, GRAM_STEP)
            mlp(0, TOP3)
            for step in range(TOP3 + 1):
                mlp(1, step)

        @block.vector
        def _(dve):
            def split(v, half, step):
                parts = xs[:, :, 0:PARTS * FH].rearrange("p d (s f) -> p s f d", s=PARTS)
                x = emb[:, half, :].rearrange("p (f d) -> p f d", d=D)
                r = rest[:, :].rearrange("p (f d) -> p f d", d=D)
                if step == 0:
                    dve.wait_ge(gathered[half], 8 * FH * (v - half) + 16 * FH)
                    nc.vector.tensor_copy(parts[:, 0], x).then_inc(split_step, 1)
                if step == 1:
                    dve.wait_ge(split_step, 3 * v + 1)
                    nc.vector.tensor_tensor(r, x, parts[:, 0], ALU.subtract).then_inc(split_step, 1)
                if step == 2:
                    dve.wait_ge(split_step, 3 * v + 2)
                    nc.vector.tensor_copy(parts[:, 1], r).then_inc(split_step, 1)
                if step == 3:
                    dve.wait_ge(split_step, 3 * v + 3)
                    nc.vector.tensor_tensor(parts[:, 2], r, parts[:, 1], ALU.subtract).then_inc(split_done, 1)

            def diagonal(v, half):
                dve.wait_ge(join_mm, v + 1)
                shape = [128, GROUPS, F, GB]
                x = misc[:, 0:GROUPS * F].rearrange("p (g f) -> p g f", g=GROUPS)
                nc.vector.tensor_tensor(xdiag[:, half, :, 0:F, :], x.unsqueeze(3).broadcast_to(shape),
                                        block_mask.unsqueeze(1).unsqueeze(1).broadcast_to(shape),
                                        ALU.mult).then_inc(xdiag_done, 1)

            def sum_x1(u, half):
                here = z12[0:H, bass.ds(u * UNIT_B, UNIT_B)].rearrange("p (g b) -> p g b", g=GROUPS)
                nc.vector.tensor_reduce(here, x1[0:H, half, :].rearrange("p (g d b) -> p g b d", g=GROUPS, d=D),
                                        AX.X, ALU.add).then_inc(z1_done, 1)

            def product(u, half, t, is_first):
                if t == 0:
                    dve.wait_ge(x1_done, 4 * u + 4)
                if t < TS:
                    dve.wait_ge(spread_mm, TS * u + t + 1)
                    x = spread_ps[t % 2][:, :]
                else:
                    got = [t0 <= t < t1 for t0, t1 in DMA_STEPS].index(True)
                    dve.wait_ge(spread_in[got], 32 * u + 32)
                    x = xspread[:, t - TS, :]
                if t >= RING or not is_first:
                    dve.wait_ge(x2_mm, FH * u + t - RING + 1)
                nc.vector.tensor_tensor(prod[:, t % RING, :], x, x1[:, half, :], ALU.mult).then_inc(prod_done, 1)

            def unit(u, half, is_first, is_last):
                late = FIRST_LATE if is_first else 0
                for t in range(FH):
                    if t == late and not is_last:
                        for s in range(4):
                            split(u + 1, 1 - half, s)
                    product(u, half, t, is_first)
                    if t == SUM_X1_STEP:
                        sum_x1(u, half)
                    if is_last and t == SUM_Z3_STEP:
                        sum_z3(0)
                    if t == DIAGONAL_STEP and not is_last:
                        diagonal(u + 1, 1 - half)

            def sum_z3(n):
                u0, un = BATCHES[n]
                cols = slice(UNIT_B * u0, UNIT_B * (u0 + un))
                dve.wait_ge(z3_half, n + 1)
                nc.vector.tensor_tensor(z3d[0:H, cols], x1_ps[0:H, 0:UNIT_B * un], z3d[0:H, cols],
                                        ALU.add).then_inc(z3_done, 1)

            dve.wait_ge(sel_in, 16)
            nc.vector.tensor_copy(sel[:, :], sel_f32[:, :]).then_inc(sel_done, 1)
            dve.wait_ge(cf_in, 16)
            for p in range(2):
                nc.vector.tensor_copy(xdiag[:, p, :, F, :],
                                      block_mask.unsqueeze(1).broadcast_to([128, GROUPS, GB])).then_inc(ones_done, 1)
            for s in range(4):
                split(0, 0, s)
            dve.wait_ge(xf_mm, 1)
            for c in range(2):
                nc.vector.tensor_copy(xf[:, CHUNK * c:CHUNK * (c + 1)], misc[64 * c:64 * c + F, :]).then_inc(xf_done, 1)
            diagonal(0, 0)
            dve.wait_ge(x1_mm, 1)
            for q in range(2):
                nc.vector.tensor_copy(x1[H * q:H * q + H, 0, CHUNK:], x1_ps[H:2 * H, :]).then_inc(x1_done, 1)
            all_units(dve, unit)
            sum_z3(1)



def constants():
    pairs = [(i, j) for i in range(F) for j in range(i, F)]
    fold = np.zeros((F * F, PAIRS), np.float32)
    add = np.zeros((F, PAIRS), np.float32)
    for m, (i, j) in enumerate(pairs):
        add[i, m] = add[j, m] = 1
        if i != j:
            fold[i * F + j, m] = fold[j * F + i, m] = 0.5
        else:
            fold[i * F:(i + 1) * F, m] = -0.5
            fold[i::F, m] = -0.5
            fold[i * F + i, m] = 1
    spread = np.zeros((F, TS, 128), np.float32)
    for t in range(TS):
        spread[t, t, 0:H] = spread[t + FH, t, H:] = 1
    by_feature = np.concatenate([add, spread.reshape(F, -1), np.eye(F, dtype=np.float32)], axis=1)
    sel = np.zeros((128, C_SEL), np.float32)
    for q in range(2):
        sel[64 * q:64 * q + PARTS * FH, 0:C_EYE] = np.tile(by_feature[FH * q:FH * q + FH], (PARTS, 1))
        sel[64 * q:64 * q + 64, C_EYE:] = np.eye(64)
    const_f32 = np.zeros((128, C_F32), np.float32)
    const_f32[:, 0:128] = np.eye(128)
    const_f32[:, 128:] = np.tile(np.eye(GB), (D, 1))
    return fold, sel, const_f32


def kernel(**inputs):
    import concourse.bacc as bacc
    from concourse.bass_utils import run_bass_kernel_spmd as run

    nc = bacc.Bacc("TRN2", target_bir_lowering=False, num_devices=1)
    arrays = {n: np.ascontiguousarray(x) for n, x in inputs.items()}
    arrays["dense_t"] = np.ascontiguousarray(arrays.pop("dense_ctx").T)
    tables = [arrays.pop(f"tbl_{f}") for f in range(F)]
    first = np.cumsum([0] + [t.shape[0] for t in tables[:-1]]).astype(np.int32)
    arrays["tables"] = np.concatenate(tables, axis=0)
    ids = arrays.pop("ids").reshape(UNITS, UNIT_B, 2, FH).transpose(2, 1, 0, 3).reshape(128, UNITS * FH)
    arrays["lookup"] = np.concatenate([ids, np.repeat(first.reshape(2, FH), UNIT_B, axis=0)], axis=1)
    for name in ("W_top3", "b_top1", "b_top2"):
        arrays[name] = np.ascontiguousarray(arrays[name].reshape(-1, 128).T)
    arrays["const_fold"], arrays["const_sel"], arrays["const_f32"] = constants()
    args = {n: nc.dram_tensor(n, x.shape, mybir.dt.from_np(x.dtype), kind="ExternalInput").ap()
            for n, x in arrays.items()}
    out = nc.dram_tensor("out", (B, 1), F32, kind="ExternalOutput").ap()
    dlrm_tower(nc, args, out)
    r = run(nc, [arrays], core_ids=[0])
    return r.results[0]["out"]
```
